# Optimizing a Trainium2 kernel written in Bass

```python
import numpy as np
import jax
import jax.numpy as jnp

def _softmax(x, axis=-1):
    return jax.nn.softmax(x, axis=axis)

def _gelu(x):
    return jax.nn.gelu(x, approximate=True)

def _silu(x):
    return jax.nn.silu(x)

def _sigmoid(x):
    return jax.nn.sigmoid(x)

def _layernorm(x, axis=-1, eps=1e-05):
    m = jnp.mean(x, axis=axis, keepdims=True)
    v = jnp.var(x, axis=axis, keepdims=True)
    return (x - m) / jnp.sqrt(v + eps)

def _scatter_add(tgt, idx, src, axis=0):
    return tgt.at[idx].add(src)

def _segment_sum(src, seg, n):
    return jax.ops.segment_sum(src, seg, n)
kernel_name = 'mk_gnn_ffn_d1_gnn_r8_4ca9d3'

def setup_inputs(seed: int=0):
    np.random.seed(seed)
    _w = jnp.asarray

    def _rec_inputs():
        import jax
        import jax.numpy as jnp
        _gk = jax.random.key(seed)
        x = -0.0006008 + 1.001 * jax.random.normal(jax.random.fold_in(_gk, 1), (6250, 256), jnp.float32)
        _s = jax.random.randint(jax.random.fold_in(_gk, 2), (100000,), 0, 6250, jnp.int32)
        _d = jax.random.randint(jax.random.fold_in(_gk, 3), (100000,), 0, 6250, jnp.int32)
        _loop = jnp.arange(6250, dtype=jnp.int32)
        src = jnp.concatenate([_s, _d, _loop])
        dst = jnp.concatenate([_d, _s, _loop])
        _o = jnp.argsort(dst, stable=True)
        src = src[_o]
        dst = dst[_o]
        edge_type_16 = jax.random.randint(jax.random.fold_in(_gk, 12), (206250,), 0, 16, jnp.int32)
        return (x, src, dst, edge_type_16)
    x, src, dst, edge_type_16 = _rec_inputs()

    def _L0_gnn_setup():
        import jax, jax.numpy as jnp
        import numpy as np
        from jax.ops import segment_sum
        N_NODES = 1250
        N_EDGES = 20000
        IN_FEAT = 256
        OUT_FEAT = 256
        NUM_RELS = 16

        def _inv_degree(idx, n):
            deg = segment_sum(jnp.ones(idx.shape[0], dtype=jnp.float32), idx, num_segments=n)
            return jnp.where(deg > 0, 1.0 / deg, 0.0)

        def _typed_pass(feat, W, bias, src_idx, dst_idx, etypes, norm_per_edge, n):
            proj = jnp.einsum('ni,rio->rno', feat, W)
            m = proj[etypes, src_idx] + bias
            m = m * norm_per_edge[:, None]
            return segment_sum(m, dst_idx, num_segments=n)
        key = jax.random.key(seed)
        ks = jax.random.split(key, 8)
        feat = jax.random.normal(ks[0], (N_NODES, IN_FEAT), dtype=jnp.float32)
        Wf = jax.random.normal(ks[1], (NUM_RELS, IN_FEAT, OUT_FEAT), dtype=jnp.float32)
        Wb = jax.random.normal(ks[2], (NUM_RELS, IN_FEAT, OUT_FEAT), dtype=jnp.float32)
        loop_weight = jax.random.normal(ks[3], (IN_FEAT, OUT_FEAT), dtype=jnp.float32)
        forward_bias = jnp.zeros((OUT_FEAT,), dtype=jnp.float32)
        backward_bias = jnp.zeros((OUT_FEAT,), dtype=jnp.float32)
        self_bias = jnp.zeros((OUT_FEAT,), dtype=jnp.float32)
        src = jax.random.randint(ks[4], (N_EDGES,), 0, N_NODES, dtype=jnp.int32)
        dst = jax.random.randint(ks[5], (N_EDGES,), 0, N_NODES, dtype=jnp.int32)
        etypes = jax.random.randint(ks[6], (N_EDGES,), 0, NUM_RELS, dtype=jnp.int32)
        return {'feat': feat, 'Wf': Wf, 'Wb': Wb, 'loop_weight': loop_weight, 'forward_bias': forward_bias, 'backward_bias': backward_bias, 'self_bias': self_bias, 'src': src, 'dst': dst, 'etypes': etypes, 'use_dis_weight': 0, 'drop_out': 0}
    _L0_gnn_all = _L0_gnn_setup()
    _L0_gnn_in = {k: v for k, v in _L0_gnn_all.items() if k in ('Wf', 'Wb', 'loop_weight', 'forward_bias', 'backward_bias', 'self_bias')}
    del _L0_gnn_all

    def _L0_ffn_setup():
        import jax, jax.numpy as jnp
        import numpy as np
        B, S, D = (8, 512, 256)
        H = 4 * D
        CAPACITY = 0.5
        key = jax.random.key(seed)
        ks = jax.random.split(key, 6)
        x = jax.random.normal(ks[0], (B, S, D), dtype=jnp.float32)
        attention_mask = jnp.zeros((B, 1, 1, S), dtype=jnp.float32)
        wr = jax.random.normal(ks[1], (D, 1), dtype=jnp.float32) * 0.02
        br = jnp.zeros((1,), dtype=jnp.float32)
        w1 = jax.random.normal(ks[2], (D, H), dtype=jnp.float32) * 0.02
        b1 = jnp.zeros((H,), dtype=jnp.float32)
        w2 = jax.random.normal(ks[3], (H, D), dtype=jnp.float32) * 0.02
        b2 = jnp.zeros((D,), dtype=jnp.float32)
        return {'x': x, 'attention_mask': attention_mask, 'wr': wr, 'br': br, 'w1': w1, 'b1': b1, 'w2': w2, 'b2': b2}
    _L0_ffn_all = _L0_ffn_setup()
    _L0_ffn_in = {k: v for k, v in _L0_ffn_all.items() if k in ('attention_mask', 'wr', 'br', 'w1', 'b1', 'w2', 'b2')}
    del _L0_ffn_all
    return {'x': x, 'src': src, 'dst': dst, 'edge_type_16': edge_type_16, 'L0_gnn_Wf': _L0_gnn_in['Wf'], 'L0_gnn_Wb': _L0_gnn_in['Wb'], 'L0_gnn_loop_weight': _L0_gnn_in['loop_weight'], 'L0_gnn_forward_bias': _L0_gnn_in['forward_bias'], 'L0_gnn_backward_bias': _L0_gnn_in['backward_bias'], 'L0_gnn_self_bias': _L0_gnn_in['self_bias'], 'L0_ffn_attention_mask': _L0_ffn_in['attention_mask'], 'L0_ffn_wr': _L0_ffn_in['wr'], 'L0_ffn_br': _L0_ffn_in['br'], 'L0_ffn_w1': _L0_ffn_in['w1'], 'L0_ffn_b1': _L0_ffn_in['b1'], 'L0_ffn_w2': _L0_ffn_in['w2'], 'L0_ffn_b2': _L0_ffn_in['b2']}

def reference(x, src, dst, edge_type_16, L0_gnn_Wf, L0_gnn_Wb, L0_gnn_loop_weight, L0_gnn_forward_bias, L0_gnn_backward_bias, L0_gnn_self_bias, L0_ffn_attention_mask, L0_ffn_wr, L0_ffn_br, L0_ffn_w1, L0_ffn_b1, L0_ffn_w2, L0_ffn_b2):
    import jax
    import jax.numpy as jnp

    def _L0_gnn_ref(feat, Wf, Wb, loop_weight, forward_bias, backward_bias, self_bias, src, dst, etypes, use_dis_weight, drop_out):
        import jax, jax.numpy as jnp
        import numpy as np
        from jax.ops import segment_sum
        N_NODES = 1250
        N_EDGES = 20000
        IN_FEAT = 256
        OUT_FEAT = 256
        NUM_RELS = 16

        def _inv_degree(idx, n):
            deg = segment_sum(jnp.ones(idx.shape[0], dtype=jnp.float32), idx, num_segments=n)
            return jnp.where(deg > 0, 1.0 / deg, 0.0)

        def _typed_pass(feat, W, bias, src_idx, dst_idx, etypes, norm_per_edge, n):
            proj = jnp.einsum('ni,rio->rno', feat, W)
            m = proj[etypes, src_idx] + bias
            m = m * norm_per_edge[:, None]
            return segment_sum(m, dst_idx, num_segments=n)
        n = feat.shape[0]
        norm_f = _inv_degree(dst, n)[dst]
        m_forward = _typed_pass(feat, Wf, forward_bias, src, dst, etypes, norm_f, n)
        norm_b = _inv_degree(src, n)[src]
        m_backward = _typed_pass(feat, Wb, backward_bias, dst, src, etypes, norm_b, n)
        s = feat @ loop_weight
        s = s + s + self_bias
        return s + m_forward + m_backward

    def _L0_ffn_ref(x, attention_mask, wr, br, w1, b1, w2, b2):
        import jax, jax.numpy as jnp
        import numpy as np
        B, S, D = (8, 512, 256)
        H = 4 * D
        CAPACITY = 0.5
        b, s, d = x.shape
        weights = (jnp.einsum('bsd,do->bso', x, wr) + br)[..., 0]
        k = max(1, int(CAPACITY * s))
        kk = k - 1 if k > 1 else 1
        _, idx = jax.lax.top_k(weights, k)
        sel_idx = idx[:, :kk]
        sel = jnp.take_along_axis(x, sel_idx[:, :, None], axis=1)
        h = jax.nn.gelu(jnp.einsum('bkd,dh->bkh', sel, w1) + b1)
        y = jnp.einsum('bkh,hd->bkd', h, w2) + b2
        w_sel = jnp.take_along_axis(weights, sel_idx, axis=1)
        y = y * w_sel[..., None]
        batch_idx = jnp.arange(b)[:, None]
        processed = jnp.zeros_like(x).at[batch_idx, sel_idx].set(y)
        return processed + x
    x = x + _L0_gnn_ref(_layernorm(x, axis=-1), L0_gnn_Wf, L0_gnn_Wb, L0_gnn_loop_weight, L0_gnn_forward_bias, L0_gnn_backward_bias, L0_gnn_self_bias, src, dst, edge_type_16, 0, 0)
    x = x + _L0_ffn_ref(_layernorm(x, axis=-1)[None], L0_ffn_attention_mask, L0_ffn_wr, L0_ffn_br, L0_ffn_w1, L0_ffn_b1, L0_ffn_w2, L0_ffn_b2)[0]
    return x

_drawn_inputs = setup_inputs


def setup_inputs(seed=0):
    import zlib

    import numpy as np

    out = dict(_drawn_inputs(seed))
    spreads = {'L0_gnn_forward_bias': (0.0, 2.0),
     'L0_gnn_backward_bias': (0.0, 2.0),
     'L0_gnn_self_bias': (0.0, 2.0),
     'L0_ffn_b1': (0.0, 0.8),
     'L0_ffn_b2': (0.0, 0.8)}
    factors = {'L0_ffn_wr': 8.0, 'L0_ffn_w1': 8.0, 'L0_ffn_w2': 8.0}
    for name, (base, spread) in spreads.items():
        noise = np.random.default_rng([zlib.crc32(name.encode()), seed]).standard_normal(out[name].shape)
        drawn = base * np.exp(spread * noise) if base else spread * noise
        out[name] = jnp.asarray(drawn.astype(out[name].dtype))
    for name, factor in factors.items():
        out[name] = (out[name] * factor).astype(out[name].dtype)
    return out
```

```python
from contextlib import ExitStack

import numpy as np

import concourse.bass as bass
from concourse import mybir

F32 = mybir.dt.float32
BF16 = mybir.dt.bfloat16
I32 = mybir.dt.int32
ALU = mybir.AluOpType
ACT = mybir.ActivationFunctionType
AX = mybir.AxisListType

P = 128

TOP = 0x40000000
ROW_BITS = 17
LANE_BITS = 11
LANE = 1 << LANE_BITS
TILES = 34
HALF = TILES // 2
HIST = 336
EPS = 1e-5


def bits_as_float(v):
    return float(np.array([v], np.uint32).view(np.float32)[0])


def gnn_ffn_kernel(nc, x, src, dst, etype, wf, wb, loop_w, fwd_bias, bwd_bias, self_bias,
                   wr, br, w1, b1, w2, b2, table_f, table_b, out):
    N, D = x.shape
    E = src.shape[0]
    R = wf.shape[0]
    H = w1.shape[1]
    NB = -(-N // P)
    LAST = N - (NB - 1) * P
    KC = D // P
    HC = H // P
    PAD_ROW = N * R
    EP = 125
    EC = E // EP
    PADS = P - 1
    PASSES = NB
    KEYS = 107 * 16
    K_TOP = max(1, N // 2) - 1
    assert EP * EC == E and EC + PADS <= LANE and N <= 1 << 13 and D == 256
    assert PASSES * TILES * P >= E + NB * PADS and KEYS >= (PASSES + 1) * TILES
    SENTINEL = TOP | (NB << 24) | PAD_ROW
    PB = R * D // 512
    WAYS = 15

    with ExitStack() as ctx:
        def sb(name, shape, dt=F32):
            return ctx.enter_context(nc.sbuf_tensor(name, shape, dt))

        def pb(name, shape, dt=F32):
            return ctx.enter_context(nc.psum_tensor(name, shape, dt))

        def sem(name):
            return ctx.enter_context(nc.semaphore(name))

        h = sb("h", [P, NB, D])
        acc_mem = sb("acc_mem", [P, NB * (D + 1)])
        acc = acc_mem[:, :].rearrange("p (b c) -> p b c", c=D + 1)
        skeys = acc_mem[:, 0:2 * LANE].rearrange("p (a f) -> p a f", a=2)
        skeys_i = skeys.bitcast(I32)
        work = [acc_mem[:, (2 + a) * LANE:(3 + a) * LANE] for a in range(2)]
        work_i = [w.bitcast(I32) for w in work]
        typ_i = acc_mem[:, 4 * LANE:4 * LANE + EC].bitcast(I32)
        xt2 = acc_mem[:, 0:KC * NB * P].rearrange("p (c n) -> p c n", c=KC)
        w_mem = sb("w_mem", [P, KC * R * D])
        wrel = w_mem[:, :].rearrange("p (c r o) -> p c r o", c=KC, r=R)
        w1_sb = w_mem[:, 0:KC * H].rearrange("p (c m) -> p c m", c=KC)
        w2_sb = w_mem[:, KC * H:KC * H + HC * D].rearrange("p (c o) -> p c o", c=HC)
        g_mem = sb("g_mem", [P, HALF * (D + 1)])
        grow = g_mem[:, :].rearrange("p (s c) -> p s c", c=D + 1)
        hot_hi = g_mem[:, 0:HIST * 8].bitcast(BF16).rearrange("p (a c v) -> p a c v", a=2, v=8)
        oh_mem = sb("oh_mem", [P, 2 * HALF * P])
        onehot = oh_mem[:, :].rearrange("p (a s n) -> p a s n", a=2, s=HALF)
        hot_lo = oh_mem[:, 0:HIST * 8].bitcast(BF16).rearrange("p (a c v) -> p a c v", a=2, v=8)
        hid = oh_mem[:, 0:HC * 512].rearrange("p (c n) -> p c n", c=HC)
        stage = sb("stage", [P, 2, R * D // 2])
        keys = sb("keys", [P, PASSES * TILES + KEYS], I32)
        ends_i = [keys[:, a * EC:(a + 1) * EC] for a in range(2)]
        loop_sb = sb("loop_sb", [P, KC, D])
        ident = sb("ident", [P, P])
        iota_f = sb("iota_f", [P, P])
        tri = sb("tri", [P, P])
        xh = sb("xh", [P, 2, D])
        xt = sb("xt", [P, KC, P])
        bias_bc = sb("bias_bc", [P, 4, D])
        iota_i = sb("iota_i", [P, P], I32)
        small_i = sb("small_i", [P, 16], I32)
        sgn = sb("sgn", [P, 8])
        sgn2 = sb("sgn2", [P, 8])
        blkmask = xh[:, 0, 0:P]
        sel_hi = stage[:, 0, 0:64]
        sel_lo = stage[:, 0, 64:128]
        ones = sb("ones", [P, P])
        hist_s = stage[:, 0, 128:256]
        hist_c = stage[:, 0, 256:320]
        pad_i = stage[:, 0, 320:448].bitcast(I32)
        padn = sb("padn", [P, 4])
        stats = stage[:, 1, 0:NB * 6].rearrange("p (b c) -> p b c", c=6)
        mv = sb("mv", [P, NB, 2])
        mneg = sb("mneg", [P, NB])
        rstd = sb("rstd", [P, NB])
        lt = sb("lt", [P, NB])
        rows_i = sb("rows_i", [P, 2, HALF + 3], I32)
        loc_i = sb("loc_i", [P, 2, HALF + 3], I32)
        loc_f = sb("loc_f", [P, 2, HALF + 3])
        pad_f = sb("pad_f", [P, 2, HALF + 3])
        blk_i = sb("blk_i", [1, 2, HALF + 3], I32)
        late_at = [0]

        def late(*shape):
            size = int(np.prod(shape))
            at = g_mem[:, late_at[0]:late_at[0] + size]
            late_at[0] += size
            return at if len(shape) == 1 else at.rearrange("p (a b) -> p a b", a=shape[0])

        inv = sb("inv", [P, NB])
        has = sb("has", [P, NB])
        wts = late(NB)
        key_i = late(2, NB).bitcast(I32)
        key_f = late(2, NB)
        cmp_f = stage[:, 0, 0:WAYS * NB].rearrange("p (w b) -> p w b", w=WAYS)
        cnt_f = late(2, WAYS)
        steps_f = late(WAYS + 1)
        thr = sb("thr", [P, 4])
        tie = late(4, NB)
        wr_sb = sb("wr_sb", [P, KC])
        b1_sb = sb("b1_sb", [P, HC])
        br_sb = sb("br_sb", [P, 1])
        wsel = late(NB)
        ybuf = late(2, D)

        bank = [pb(f"bank{n}", [P, 512]) for n in range(8)]
        ring = bank[0:4]
        pj = bank[4:6]
        ps_t = bank[6]
        ps_s = bank[7]

        names = ("x_in edges_in bias_in wf_in wb_in loop_in ffn_in const_ready dve_chain stats_ready "
                 "var_ready std_ready hot_ready hist_chunk hist_masked hist_sum hist_picked hist_total pad_counts "
                 "keys_out keys_copied sorted_ready stage_done xh_part xh_ready turned xt_ready "
                 "proj_done proj_out half_ready mm_done added self_done h_ready folded "
                 "wt_done wt_ready cmp_ready cnt_done z_ready hid_done hid_ready "
                 "y_done y_ready fin_ready gather_go blocks_go pool_const thr_done xt2_ready wt_mask").split()
        S = {n: sem(n) for n in names}
        stored = [sem("stored_lo"), sem("stored_hi")]
        stage_free = [sem("stage_free_lo"), sem("stage_free_hi")]
        gathered = [sem(f"gathered{n}") for n in range(HALF)]
        out_done = [sem("out_done0"), sem("out_done1")]

        block = ctx.enter_context(nc.Block())

        @block.sync
        def _(sp):
            for a in range(2):
                sp.sem_inc(stage_free[a], 1)
            sp.wait_ge(S["const_ready"], 1)
            sp.dma_start(h[:, 0:NB - 1, :], x[0:(NB - 1) * P, :].rearrange("(b p) d -> p b d", p=P)).then_inc(S["x_in"], 16)
            sp.dma_start(h[0:LAST, NB - 1, :], x[(NB - 1) * P:N, :]).then_inc(S["x_in"], 16)
            sp.dma_start(ends_i[0][0:EP, :], dst.rearrange("(p c) -> p c", c=EC)).then_inc(S["edges_in"], 16)
            sp.dma_start(ends_i[1][0:EP, :], src.rearrange("(p c) -> p c", c=EC)).then_inc(S["edges_in"], 16)
            sp.dma_start(typ_i[0:EP, :], etype.rearrange("(p c) -> p c", c=EC)).then_inc(S["edges_in"], 16)
            for c in range(KC):
                sp.dma_start(wrel[:, c], wf[:, c * P:(c + 1) * P, :].rearrange("r p o -> p r o")).then_inc(S["wf_in"], 16)
                sp.dma_start(loop_sb[:, c], loop_w[c * P:(c + 1) * P, :]).then_inc(S["loop_in"], 16)
                sp.dma_start(wr_sb[:, c:c + 1], wr[c * P:(c + 1) * P, :]).then_inc(S["bias_in"], 16)
            for n, b in enumerate((fwd_bias, bwd_bias, self_bias, b2)):
                sp.dma_start(bias_bc[:, n, :], b.rearrange("(a d) -> a d", a=1).broadcast_to([P, D])).then_inc(S["bias_in"], 16)
            sp.dma_start(b1_sb[:, :], b1.rearrange("(c p) -> p c", p=P), allow_slow_non_contiguous=True).then_inc(S["bias_in"], 16)
            sp.dma_start(br_sb[:, :], br.rearrange("(a d) -> a d", a=1).broadcast_to([P, 1])).then_inc(S["bias_in"], 16)

            def store_block(table, i, n):
                t = table.rearrange("(b p r) d -> b p (r d)", p=P, r=R)
                for a in range(2):
                    sp.wait_ge(S["proj_out"], n * PB + (a + 1) * (PB // 2) + 2)
                    sp.dma_start(t[bass.ds(i, 1), :, a * (R * D // 2):(a + 1) * (R * D // 2)].rearrange("a p f -> (a p) f"),
                                 stage[:, a, :]).then_inc(stored[a], 16)
                    sp.wait_ge(stored[a], (n + 1) * 16)
                    sp.sem_inc(stage_free[a], 1)

            with sp.Fori(0, NB) as i:
                store_block(table_f, i, i)
            sp.wait_ge(S["proj_done"], NB * PB)
            for c in range(KC):
                sp.dma_start(wrel[:, c], wb[:, c * P:(c + 1) * P, :].rearrange("r p o -> p r o")).then_inc(S["wb_in"], 16)
            with sp.Fori(0, NB) as i:
                store_block(table_b, i, i + NB)
            sp.wait_ge(S["proj_done"], 2 * NB * PB)
            sp.dma_start(w1_sb, w1.rearrange("(c p) m -> p c m", p=P)).then_inc(S["ffn_in"], 16)
            sp.dma_start(w2_sb, w2.rearrange("(c p) o -> p c o", p=P)).then_inc(S["ffn_in"], 16)
            with sp.Fori(0, (NB - 1) // 2) as i:
                for a in range(2):
                    sp.wait_ge(S["fin_ready"], 2 * i + a + 2)
                    sp.dma_start(out[bass.ds(i * 2 * P + a * P, P), :], h[:, bass.ds(2 * i + a, 1), :].rearrange("p a d -> p (a d)")).then_inc(out_done[a], 16)
            sp.wait_ge(S["fin_ready"], NB + 1)
            sp.dma_start(out[(NB - 1) * P:N, :], h[0:LAST, NB - 1, :]).then_inc(out_done[0], 16)
            sp.wait_ge(out_done[0], ((NB - 1) // 2 + 1) * 16)
            sp.wait_ge(out_done[1], ((NB - 1) // 2) * 16)

        @block.gpsimd
        def _(pool):
            g = nc.gpsimd
            g.memset(h[:, NB - 1, :], 0.0).then_inc(S["const_ready"], 1)
            g.iota(iota_i[:, :], pattern=[[1, P]], base=0, channel_multiplier=0).then_inc(S["pool_const"], 1)
            g.iota(small_i[:, 0:8], pattern=[[0, 8]], base=0, channel_multiplier=1).then_inc(S["pool_const"], 1)
            g.iota(pad_i[:, :], pattern=[[1, P]], base=PAD_ROW, channel_multiplier=0).then_inc(S["pool_const"], 1)
            g.memset(ident[:, :], 0.0).then_inc(S["pool_const"], 1)
            g.memset(ones[:, :], 1.0).then_inc(S["pool_const"], 1)
            pool.wait_ge(S["pool_const"], 5)
            g.affine_select(out=ident[:, :], in_=ident[:, :], compare_op=ALU.not_equal, fill=1.0,
                            base=0, pattern=[[-1, P]], channel_multiplier=1).then_inc(S["pool_const"], 1)
            g.affine_select(out=tri[:, :], in_=ones[:, :], compare_op=ALU.is_gt, fill=0.0,
                            base=0, pattern=[[1, P]], channel_multiplier=-1).then_inc(S["pool_const"], 1)
            for hot in (hot_hi, hot_lo):
                for a in range(2):
                    g.memset(hot[:, a, HIST - 6:HIST, :], 0.0).then_inc(S["pool_const"], 1)
            pool.wait_ge(S["hist_chunk"], 2 * (EC // (HIST - 6)))
            g.memset(grow[:, :, D:D + 1], 1.0).then_inc(S["pool_const"], 1)

            def gather(table, i):
                for t in range(TILES):
                    half, s = t // HALF, t % HALF
                    pool.wait_ge(S["mm_done"], TILES * i + t + 1)
                    if s == 0:
                        pool.wait_ge(S["half_ready"], 2 * i + half + 1)
                    pool.sem_inc(S["gather_go"], 1)
                    g.indirect_dma_start(grow[:, s, 0:D], None, table,
                                         bass.IndirectOffsetOnAxis(rows_i[:, half, s:s + 1], 0)).then_inc(gathered[s], 16)

            pool.wait_ge(S["pool_const"], 12)
            for a in range(2):
                pool.wait_ge(stored[a], NB * 16)
            with pool.Fori(0, PASSES) as i:
                gather(table_f, i)
            for a in range(2):
                pool.wait_ge(stored[a], 2 * NB * 16)
            with pool.Fori(PASSES, 2 * PASSES) as i:
                gather(table_b, i)

        @block.scalar
        def _(act):
            a_ = nc.scalar
            act.sem_inc(S["proj_out"], 2)
            act.sem_inc(S["xt_ready"], 1)
            act.sem_inc(S["xt2_ready"], 1)
            act.wait_ge(S["var_ready"], 1)
            a_.activation(lt[:, :], rstd[:, :], ACT.Sqrt).then_inc(S["std_ready"], 1)
            act.wait_ge(S["stats_ready"], 1)

            def norm_block(i, n):
                act.wait_ge(S["turned"], n + 1)
                a_.activation(xh[:, 0, :], h[:, bass.ds(i, 1), :].rearrange("p a d -> p (a d)"), ACT.Identity,
                              bias=mneg[:, bass.ds(i, 1)]).then_inc(S["xh_part"], 1)
                act.wait_ge(S["xh_part"], n + 1)
                a_.activation(xh[:, 1, :], xh[:, 0, :], ACT.Copy, scale=rstd[:, bass.ds(i, 1)]).then_inc(S["xh_ready"], 1)

            def project_out(i, n):
                norm_block(i, n)
                act.wait_ge(S["turned"], n + 2)
                a_.activation(xt[:, :, :].rearrange("p c n -> p (c n)"), ps_t[:, 0:KC * P], ACT.Copy).then_inc(S["xt_ready"], 1)
                for k in range(PB):
                    half, at = k // (PB // 2), k % (PB // 2) * 512
                    act.wait_ge(S["proj_done"], n * PB + k + 1)
                    if at == 0:
                        act.wait_ge(stage_free[half], n + 1)
                    a_.activation(stage[:, half, at:at + 512], pj[k % 2][:, :], ACT.Copy).then_inc(S["proj_out"], 1)

            act.wait_ge(S["pad_counts"], 2)
            with act.Fori(0, NB) as i:
                project_out(i, i)
            with act.Fori(0, NB) as i:
                project_out(i, i + NB)
            act.wait_ge(S["var_ready"], 2)
            a_.activation(lt[:, :], rstd[:, :], ACT.Sqrt).then_inc(S["std_ready"], 1)
            act.wait_ge(S["stats_ready"], 2)
            with act.Fori(0, NB) as i:
                act.wait_ge(S["z_ready"], i + 1)
                norm_block(i, i + 2 * NB)
                act.wait_ge(S["turned"], i + 2 * NB + 2)
                a_.activation(xt[:, :, :].rearrange("p c n -> p (c n)"), ps_t[:, 0:KC * P], ACT.Copy).then_inc(S["xt_ready"], 1)
                a_.activation(xt2[:, :, bass.ds(i * P, P)], ps_t[:, 0:KC * P].rearrange("p (c n) -> p c n", c=KC),
                              ACT.Copy).then_inc(S["xt2_ready"], 1)

            def hidden(n, base, width):
                for m in range(HC):
                    act.wait_ge(S["hid_done"], base + m + 1)
                    a_.activation(hid[:, m, 0:width], bank[m % 2][:, 0:width], ACT.Gelu_apprx_tanh,
                                  bias=b1_sb[:, m:m + 1]).then_inc(S["hid_ready"], 1)

            with act.Fori(0, (NB - 1) // 4) as i:
                act.wait_ge(S["y_done"], 4 * i + 1)
                hidden(i, i * HC, 4 * P)
            act.wait_ge(S["y_done"], NB)
            hidden((NB - 1) // 4, (NB - 1) // 4 * HC, P)

        @block.vector
        def _(dve):
            v = nc.vector
            links = [0]
            for name in ("h_ready", "fin_ready", "z_ready"):
                dve.sem_inc(S[name], 1)

            def link(*ins):
                for x_ in ins:
                    links[0] += 1
                    x_.then_inc(S["dve_chain"], 1)
                dve.wait_ge(S["dve_chain"], links[0])

            dve.wait_ge(S["pool_const"], 11)
            link(v.memset(skeys[:, :, :], bits_as_float(SENTINEL)),
                 v.tensor_copy(iota_f[:, :], iota_i[:, :]))

            def statistics(b):
                return v.bn_stats(stats[:, b, :], h[:, b, :])

            def finish_statistics(n):
                link(v.tensor_scalar(mneg[:, :], mv[:, :, 0], -1.0, None, ALU.mult),
                     v.tensor_scalar(rstd[:, :], mv[:, :, 1], 1.0, EPS, ALU.mult, ALU.add))
                v.tensor_copy(mv[:, :, 1], rstd[:, :]).then_inc(S["var_ready"], 1)
                dve.wait_ge(S["std_ready"], n)
                dve.wait_ge(S["var_ready"], n)
                link(v.reciprocal(rstd[:, :], lt[:, :]))
                link(v.tensor_tensor(lt[:, :], rstd[:, :], rstd[:, :], ALU.mult))
                link(v.tensor_tensor(lt[:, :], lt[:, :], mv[:, :, 1], ALU.mult))
                link(v.tensor_scalar(lt[:, :], lt[:, :], -0.5, 1.5, ALU.mult, ALU.add))
                link(v.tensor_tensor(rstd[:, :], rstd[:, :], lt[:, :], ALU.mult))
                v.tensor_copy(stats[:, 0, 0:1], rstd[:, 0:1]).then_inc(S["stats_ready"], 1)

            dve.wait_ge(S["x_in"], 32)
            link(*[statistics(b) for b in range(NB)])
            link(*[v.bn_aggr(mv[:, b, :], stats[:, b, :]) for b in range(NB)])
            finish_statistics(1)

            link(*[v.tensor_scalar(small_i[:, 8 + b:9 + b], small_i[:, b:b + 1], b, 1,
                                   ALU.logical_shift_right, ALU.bitwise_and) for b in range(7)])
            link(v.tensor_scalar(sgn[:, 0:7], small_i[:, 8:15], -2.0, 1.0, ALU.mult, ALU.add))
            link(v.tensor_tensor(sgn2[:, 1:7], sgn[:, 0:6], sgn[:, 1:7], ALU.mult))
            link(v.tensor_scalar(hist_s[:, :].bitcast(I32), iota_i[:, :], 3, None, ALU.logical_shift_right),
                 v.tensor_scalar(small_i[:, 8:9], small_i[:, 0:1], 3, None, ALU.logical_shift_right),
                 v.tensor_scalar(small_i[:, 9:10], small_i[:, 0:1], 7, None, ALU.bitwise_and),
                 v.tensor_scalar(hist_c[:, :].bitcast(I32), iota_i[:, 0:64], 7, None, ALU.bitwise_and))
            link(v.tensor_copy(padn[:, 0:2], small_i[:, 8:10]),
                 v.tensor_copy(iota_f[:, :], hist_s[:, :].bitcast(I32)),
                 v.tensor_copy(sel_lo, hist_c[:, :].bitcast(I32)))
            link(v.tensor_scalar(blkmask, iota_f[:, :], padn[:, 0:1], None, ALU.is_equal),
                 v.tensor_scalar(sel_hi, iota_f[:, 0:64], padn[:, 1:2], None, ALU.is_equal),
                 v.tensor_scalar(sel_lo, sel_lo, padn[:, 1:2], None, ALU.is_equal))
            link(v.tensor_copy(iota_f[:, :], iota_i[:, :]))

            dve.wait_ge(S["edges_in"], 48)
            W = HIST - 6
            for d in range(2):
                node = ends_i[d][0:EP, :]
                link(v.tensor_scalar(work_i[0][0:EP, 0:EC], node, 10, None, ALU.logical_shift_right),
                     v.tensor_scalar(work_i[1][0:EP, 0:EC], node, 7, 7, ALU.logical_shift_right, ALU.bitwise_and))
                for c in range(EC // W):
                    n = d * (EC // W) + c
                    if n >= 2:
                        dve.wait_ge(S["hist_chunk"], n - 1)
                    for digit, hot in ((0, hot_hi), (1, hot_lo)):
                        v.tensor_tensor(hot[0:EP, n % 2, 0:W, :],
                                        work_i[digit][0:EP, c * W:(c + 1) * W].unsqueeze(2).broadcast_to([EP, W, 8]),
                                        iota_f[0:EP, 0:8].unsqueeze(1).broadcast_to([EP, W, 8]),
                                        ALU.is_equal).then_inc(S["hot_ready"], 1)
                dve.wait_ge(S["hot_ready"], 2 * (d + 1) * (EC // W))
            for d in range(2):
                dve.wait_ge(S["hist_chunk"], 2 * (EC // W))
                v.tensor_tensor(hist_s[:, :], bank[d][:, 0:P], blkmask, ALU.mult).then_inc(S["hist_masked"], 1)
                dve.wait_ge(S["hist_sum"], d + 1)
                v.tensor_tensor(hist_c[:, :], bank[2][:, 0:64], sel_lo, ALU.mult).then_inc(S["hist_picked"], 1)
                dve.wait_ge(S["hist_total"], d + 1)
                link(v.tensor_scalar(small_i[0:64, 8:9], bank[3][0:64, 0:1], -1.0, None, ALU.mult))
                link(v.tensor_scalar(small_i[0:64, 9:10], small_i[0:64, 8:9], P - 1, None, ALU.bitwise_and))
                link(v.tensor_copy(padn[0:64, 0:1], small_i[0:64, 9:10]))
                link(v.tensor_scalar(small_i[0:64, 10:11], small_i[0:64, 0:1], 24, TOP, ALU.logical_shift_left, ALU.bitwise_or))
                link(v.tensor_tensor(hist_s[0:64, :].bitcast(I32), pad_i[0:64, :],
                                     small_i[0:64, 10:11].broadcast_to([64, P]), ALU.bitwise_or),
                     v.tensor_scalar(work[0][0:64, 0:P], iota_f[0:64, :], padn[0:64, 0:1], None, ALU.is_lt))
                link(v.copy_predicated(skeys[0:NB, d, EC:EC + PADS], work_i[0][0:NB, 0:PADS],
                                       hist_s[0:NB, 0:PADS]))
                link(v.tensor_scalar(work_i[0][0:EP, 0:EC], ends_i[d][0:EP, :], ROW_BITS, TOP,
                                     ALU.logical_shift_left, ALU.bitwise_or),
                     v.tensor_scalar(work_i[1][0:EP, 0:EC], ends_i[1 - d][0:EP, :], 4, None, ALU.logical_shift_left))
                link(v.tensor_tensor(work_i[0][0:EP, 0:EC], work_i[0][0:EP, 0:EC], work_i[1][0:EP, 0:EC], ALU.bitwise_or))
                link(v.tensor_tensor(skeys_i[0:EP, d, 0:EC], work_i[0][0:EP, 0:EC], typ_i[0:EP, :], ALU.bitwise_or))
            v.tensor_copy(padn[:, 2:3], iota_f[:, 0:1]).then_inc(S["pad_counts"], 2)

            done = S["stage_done"]
            with dve.Fori(0, 2) as d:
                count = 0
                flips = 0
                lanes = skeys[:, bass.ds(d, 1), :].rearrange("p a f -> p (a f)")
                cur = lanes

                def other():
                    nonlocal flips
                    flips += 1
                    return work[flips % 2]

                def put(ins):
                    nonlocal count
                    count += 1
                    ins.then_inc(done, 1)

                def settle(now):
                    nonlocal cur
                    cur = now
                    dve.wait_ge(done, count)

                def directed(m, k):
                    to = other()
                    a, b = (y.rearrange("p (g r h t l) -> p g r h t l", r=2, h=1 << (m - 1 - k), t=2, l=1 << k)
                            for y in (cur, to))
                    for r in range(2):
                        put(v.tensor_tensor(b[:, :, r, :, r, :], a[:, :, r, :, 0, :], a[:, :, r, :, 1, :], ALU.min))
                        put(v.tensor_tensor(b[:, :, r, :, 1 - r, :], a[:, :, r, :, 0, :], a[:, :, r, :, 1, :], ALU.max))
                    settle(to)

                def ascend(k, to=None):
                    to = other() if to is None else to
                    a, b = (y.rearrange("p (h t l) -> p h t l", t=2, l=1 << k) for y in (cur, to))
                    put(v.tensor_tensor(b[:, :, 0, :], a[:, :, 0, :], a[:, :, 1, :], ALU.min))
                    put(v.tensor_tensor(b[:, :, 1, :], a[:, :, 0, :], a[:, :, 1, :], ALU.max))
                    settle(to)

                def negate(sign):
                    to = other()
                    put(v.tensor_scalar(to, cur, sign, None, ALU.mult))
                    settle(to)

                def turn():
                    to = other()
                    put(v.transpose(to, cur))
                    settle(to)

                def quadrants(bit):
                    to = other()
                    for q in range(4):
                        w = q ^ bit
                        put(v.tensor_scalar(to[32 * q:32 * q + 32], cur[32 * w:32 * w + 32], -1.0, None, ALU.mult))
                    settle(cur)
                    put(v.tensor_tensor(to, cur, to, ALU.min))
                    settle(to)

                for m in range(1, LANE_BITS):
                    for k in reversed(range(m)):
                        directed(m, k)
                negate(sgn[:, 0:1])
                for k in reversed(range(LANE_BITS)):
                    ascend(k)
                for m in range(LANE_BITS + 1, LANE_BITS + 8):
                    if m <= 16:
                        negate(sgn2[:, m - 11:m - 10])
                    elif m == 17:
                        negate(sgn[:, 6:7])
                        quadrants(1)
                        negate(sgn[:, 5:6])
                    else:
                        quadrants(2)
                        negate(sgn2[:, 6:7])
                        quadrants(1)
                        negate(sgn[:, 5:6])
                    turn()
                    for k in reversed(range(LANE_BITS, min(m, 16))):
                        ascend(k - LANE_BITS)
                    for k in reversed(range(5, LANE_BITS)):
                        ascend(k)
                    turn()
                    for k in reversed(range(5)):
                        ascend(k, lanes if m == 18 and k == 0 else None)
                dve.sem_clear(done)
                v.tensor_copy(small_i[:, 8:9], small_i[:, 0:1]).then_inc(S["sorted_ready"], 1)

            for d in range(2):
                for q in range(4):
                    dve.wait_ge(S["keys_out"], 4 * d + q + 1)
                    to = keys[:, d * PASSES * TILES:d * PASSES * TILES + KEYS].rearrange("p (r c) -> p c r", c=16)
                    v.tensor_copy(to[:, 4 * q:4 * q + 4, :],
                                  bank[q][:, :].bitcast(I32).rearrange("p (c r) -> p c r", c=4)[:, :, 0:KEYS // 16]).then_inc(S["keys_copied"], 1)
                dve.wait_ge(S["keys_copied"], 4 * (d + 1))
            link(v.memset(acc_mem[:, :], 0.0))
            dve.sem_inc(S["added"], 4)

            def stage_half(i, half, wait):
                kt = keys[:, bass.ds(i * TILES + half * HALF, HALF)]
                v.tensor_scalar(rows_i[:, half, 0:HALF], kt, (1 << ROW_BITS) - 1, None, ALU.bitwise_and).then_inc(S["cmp_ready"], 1)
                v.tensor_scalar(loc_i[:, half, 0:HALF], kt, ROW_BITS, P - 1, ALU.logical_shift_right, ALU.bitwise_and).then_inc(S["cmp_ready"], 1)
                v.tensor_scalar(blk_i[0:1, half, 0:HALF], kt[0:1, :], 24, 63,
                                ALU.logical_shift_right, ALU.bitwise_and).then_inc(S["cmp_ready"], 1)
                dve.wait_ge(S["cmp_ready"], wait + 3)
                v.tensor_scalar(pad_f[:, half, 0:HALF], rows_i[:, half, 0:HALF], float(PAD_ROW), 1000.0,
                                ALU.is_ge, ALU.mult).then_inc(S["cmp_ready"], 1)
                v.tensor_scalar(blk_i[0:1, half, 0:HALF], blk_i[0:1, half, 0:HALF], float(NB - 1), None, ALU.min).then_inc(S["cmp_ready"], 1)
                dve.wait_ge(S["cmp_ready"], wait + 5)
                v.tensor_tensor(loc_f[:, half, 0:HALF], loc_i[:, half, 0:HALF], pad_f[:, half, 0:HALF], ALU.add).then_inc(S["cmp_ready"], 1)
                dve.wait_ge(S["cmp_ready"], wait + 6)
                v.tensor_tensor(onehot[:, half, :, :], iota_f[:, :].unsqueeze(1).broadcast_to([P, HALF, P]),
                                loc_f[:, half, 0:HALF].unsqueeze(2).broadcast_to([P, HALF, P]),
                                ALU.is_equal).then_inc(S["half_ready"], 1)

            for half in range(2):
                stage_half(0, half, 6 * half)

            def add_tiles(i):
                for half in range(2):
                    dve.wait_ge(S["half_ready"], 2 * i + half + 1)
                    dve.sem_inc(S["blocks_go"], 1)
                    _, blocks = nc.values_load_multi_w_load_instructions(
                        blk_i[0:1, half, 0:HALF], engines=(mybir.EngineType.DVE,), min_val=0, max_val=NB - 1,
                        skip_runtime_bounds_check_because="the block is masked to six bits and clamped to the last one")
                    for s in range(HALF):
                        t = half * HALF + s
                        dve.wait_ge(S["mm_done"], TILES * i + t + HALF + 1)
                        dve.wait_ge(S["added"], TILES * i + t + 4)
                        to = acc[:, bass.ds(blocks[s], 1), :].rearrange("p a c -> p (a c)")
                        v.tensor_tensor(to, ring[t % 4][:, 0:D + 1], to, ALU.add).then_inc(S["added"], 1)
                    stage_half(i + 1, half, 12 * (i + 1) + 6 * half)

            def self_loop(i):
                hb = h[:, bass.ds(i, 1), :].rearrange("p a d -> p (a d)")
                dve.wait_ge(S["self_done"], i + 1)
                v.scalar_tensor_tensor(out=hb, in0=ps_s[:, 0:D], scalar=2.0, in1=hb, op0=ALU.mult, op1=ALU.add).then_inc(S["h_ready"], 1)
                dve.wait_ge(S["h_ready"], 2 * i + 2)
                v.tensor_tensor(hb, hb, bias_bc[:, 2, :], ALU.add).then_inc(S["h_ready"], 1)

            dve.wait_ge(S["bias_in"], (KC + 6) * 16)
            with dve.Fori(0, PASSES) as i:
                add_tiles(i)
                self_loop(i)

            def fold(d):
                dve.wait_ge(S["added"], (d + 1) * PASSES * TILES + 4)
                dve.wait_ge(S["h_ready"], 2 * NB + 1)
                link(v.tensor_scalar(inv[:, :], acc[:, :, D], 1.0, None, ALU.max),
                     v.tensor_scalar(has[:, :], acc[:, :, D], 1.0, None, ALU.min))
                link(v.reciprocal(inv[:, :], inv[:, :]))
                link(v.tensor_tensor(inv[:, :], inv[:, :], has[:, :], ALU.mult))
                with dve.Fori(0, NB) as i:
                    hb = h[:, bass.ds(i, 1), :].rearrange("p a d -> p (a d)")
                    at = acc[:, bass.ds(i, 1), 0:D].rearrange("p a d -> p (a d)")
                    v.scalar_tensor_tensor(out=hb, in0=at, scalar=inv[:, bass.ds(i, 1)], in1=hb,
                                           op0=ALU.mult, op1=ALU.add).then_inc(S["folded"], 1)
                    dve.wait_ge(S["folded"], 2 * (i + d * NB) + 1)
                    v.scalar_tensor_tensor(out=hb, in0=bias_bc[:, d, :], scalar=has[:, bass.ds(i, 1)], in1=hb,
                                           op0=ALU.mult, op1=ALU.add).then_inc(S["folded"], 1)
                dve.wait_ge(S["folded"], 2 * (d + 1) * NB)

            fold(0)
            link(v.memset(acc_mem[:, :], 0.0))
            with dve.Fori(PASSES, 2 * PASSES) as i:
                add_tiles(i)
            fold(1)

            link(*[statistics(b) for b in range(NB)])
            link(*[v.bn_aggr(mv[:, b, :], stats[:, b, :]) for b in range(NB)])
            finish_statistics(2)
            with dve.Fori(0, NB) as i:
                hb = h[:, bass.ds(i, 1), :].rearrange("p a d -> p (a d)")
                dve.wait_ge(S["xh_ready"], 2 * NB + i + 1)
                v.tensor_tensor(hb, hb, xh[:, 1, :], ALU.add).then_inc(S["z_ready"], 1)

            dve.wait_ge(S["wt_done"], NB)
            link(v.tensor_scalar(wts[:, :], ps_s[:, 0:NB], br_sb[:, 0:1], None, ALU.add))
            link(v.tensor_scalar(wts[:, :], wts[:, :], 0.0, None, ALU.add))
            wt_i = wts[:, :].bitcast(I32)
            link(v.tensor_scalar(key_i[:, 0, :], wt_i, 31, None, ALU.arith_shift_right))
            link(v.tensor_scalar(key_i[:, 0, :], key_i[:, 0, :], -(1 << 31), None, ALU.bitwise_or))
            link(v.tensor_tensor(key_i[:, 0, :], key_i[:, 0, :], wt_i, ALU.bitwise_xor))
            link(v.tensor_scalar(key_i[:, 1, :], key_i[:, 0, :], 0xFFFF, None, ALU.bitwise_and))
            link(v.tensor_scalar(key_i[:, 0, :], key_i[:, 0, :], 16, 0xFFFF, ALU.logical_shift_right, ALU.bitwise_and))
            link(v.tensor_copy(key_f[:, :, :], key_i[:, :, :]))
            link(v.tensor_scalar(key_f[:, 0, NB - 1:NB], key_f[:, 0, NB - 1:NB], 1.0, None, ALU.add))
            link(v.tensor_scalar(thr[:, 2:3], small_i[:, 0:1], float(LAST), None, ALU.is_lt))
            link(v.tensor_scalar(key_f[:, 0, NB - 1:NB], key_f[:, 0, NB - 1:NB], thr[:, 2:3], -1.0, ALU.mult, ALU.add))
            link(v.tensor_scalar(steps_f[:, 0:WAYS], iota_f[:, 1:WAYS + 1], 1.0, None, ALU.mult))
            rounds = 0
            for phase in range(2):
                if phase == 1:
                    link(v.tensor_scalar(tie[:, 0, :], key_f[:, 0, :], thr[:, 0:1], None, ALU.is_equal),
                         v.tensor_scalar(tie[:, 1, :], key_f[:, 0, :], thr[:, 0:1], 65537.0, ALU.is_gt, ALU.mult),
                         v.tensor_scalar(tie[:, 2, :], key_f[:, 1, :], 1.0, None, ALU.add))
                    link(v.tensor_tensor(tie[:, 0, :], tie[:, 0, :], tie[:, 2, :], ALU.mult))
                    link(v.tensor_tensor(tie[:, 0, :], tie[:, 0, :], tie[:, 1, :], ALU.add))
                    link(v.tensor_scalar(key_f[:, 0, :], tie[:, 0, :], -1.0, None, ALU.add))
                link(v.memset(thr[:, 0:1], 0.0))
                for step in (4096.0, 256.0, 16.0, 1.0):
                    link(v.tensor_scalar(cnt_f[:, 0, :], steps_f[:, 0:WAYS], step, thr[:, 0:1], ALU.mult, ALU.add))
                    link(v.tensor_tensor(cmp_f, key_f[:, 0, :].unsqueeze(1).broadcast_to([P, WAYS, NB]),
                                         cnt_f[:, 0, :].unsqueeze(2).broadcast_to([P, WAYS, NB]), ALU.is_ge))
                    v.tensor_reduce(cnt_f[:, 1, :], cmp_f, AX.X, ALU.add).then_inc(S["wt_ready"], 1)
                    rounds += 1
                    dve.wait_ge(S["cnt_done"], rounds)
                    link(v.tensor_scalar(cnt_f[:, 1, :], ps_t[:, 0:WAYS], float(K_TOP), step, ALU.is_ge, ALU.mult))
                    link(v.tensor_reduce(thr[:, 1:2], cnt_f[:, 1, :], AX.X, ALU.add))
                    link(v.tensor_tensor(thr[:, 0:1], thr[:, 0:1], thr[:, 1:2], ALU.add))
            link(v.tensor_scalar(tie[:, 0, :], key_f[:, 0, :], thr[:, 0:1], None, ALU.is_gt))
            v.tensor_scalar(tie[:, 1, :], key_f[:, 0, :], thr[:, 0:1], None, ALU.is_equal).then_inc(S["wt_ready"], 1)
            rounds += 1
            dve.wait_ge(S["cnt_done"], rounds)
            link(v.tensor_reduce(thr[:, 1:2], ps_t[:, 0:NB], AX.X, ALU.add),
                 v.tensor_copy(tie[:, 2, :], ps_t[:, NB:2 * NB]),
                 v.memset(key_f[:, 1, :], 0.0))
            link(v.tensor_scalar(thr[:, 1:2], thr[:, 1:2], -1.0, float(K_TOP), ALU.mult, ALU.add),
                 v.tensor_tensor_scan(tie[:, 3, :], tie[:, 2, :], key_f[:, 1, :], 0.0, ALU.add, ALU.add))
            link(v.tensor_tensor(tie[:, 3, :], tie[:, 3, :], tie[:, 2, :], ALU.subtract))
            link(v.tensor_tensor(tie[:, 3, :], tie[:, 3, :], ps_t[:, 2 * NB:3 * NB], ALU.add))
            link(v.tensor_scalar(tie[:, 3, :], tie[:, 3, :], thr[:, 1:2], None, ALU.is_lt))
            link(v.tensor_tensor(tie[:, 3, :], tie[:, 3, :], tie[:, 1, :], ALU.mult))
            link(v.tensor_tensor(tie[:, 3, :], tie[:, 3, :], tie[:, 0, :], ALU.add))
            link(v.tensor_tensor(wsel[:, :], tie[:, 3, :], wts[:, :], ALU.mult))
            v.tensor_copy(thr[:, 3:4], thr[:, 1:2]).then_inc(S["thr_done"], 1)

            def finish_block(i, q):
                hb = h[:, bass.ds(i, 1), :].rearrange("p a d -> p (a d)")
                dve.wait_ge(S["y_done"], i + 2)
                v.tensor_tensor(ybuf[:, q % 2, :], bank[4 + q][:, 0:D], bias_bc[:, 3, :], ALU.add).then_inc(S["y_ready"], 1)
                dve.wait_ge(S["y_ready"], i + 1)
                v.scalar_tensor_tensor(out=hb, in0=ybuf[:, q % 2, :], scalar=wsel[:, bass.ds(i, 1)], in1=hb,
                                       op0=ALU.mult, op1=ALU.add).then_inc(S["fin_ready"], 1)

            dve.wait_ge(S["z_ready"], NB + 1)
            with dve.Fori(0, (NB - 1) // 4) as i:
                for q in range(4):
                    if q:
                        dve.wait_ge(S["fin_ready"], 4 * i + q + 1)
                    finish_block(4 * i + q, q)
            dve.wait_ge(S["fin_ready"], NB)
            finish_block(NB - 1, 0)

        @block.tensor
        def _(pe):
            te = nc.tensor
            pe.sem_inc(S["mm_done"], HALF)
            pe.sem_inc(S["turned"], 1)
            pe.sem_inc(S["y_done"], 1)
            W = HIST // 16
            pe.wait_ge(S["pool_const"], 11)
            for d in range(2):
                for c in range(5):
                    n = 5 * d + c
                    pe.wait_ge(S["hot_ready"], 2 * n + 2)
                    for k in range(W):
                        last = te.matmul(bank[d][:, 0:P], hot_hi[0:EP, n % 2, 16 * k:16 * k + 16, :].rearrange("p c v -> p (c v)"),
                                         hot_lo[0:EP, n % 2, 16 * k:16 * k + 16, :].rearrange("p c v -> p (c v)"),
                                         start=c == 0 and k == 0, stop=c == 4 and k == W - 1)
                    last.then_inc(S["hist_chunk"], 1)
            for d in range(2):
                pe.wait_ge(S["hist_masked"], d + 1)
                te.matmul(bank[2][:, 0:64], hist_s[:, :], sel_hi, start=True, stop=True).then_inc(S["hist_sum"], 1)
                pe.wait_ge(S["hist_picked"], d + 1)
                te.matmul(bank[3][0:64, 0:1], hist_c[:, :], ones[:, 0:1], start=True, stop=True).then_inc(S["hist_total"], 1)

            def turn_block(n):
                pe.wait_ge(S["xh_ready"], n + 1)
                for c in range(KC):
                    last = te.transpose(ps_t[:, c * P:(c + 1) * P], xh[:, 1, c * P:(c + 1) * P], ident[:, :])
                last.then_inc(S["turned"], 1)

            def project_bank(n, k):
                pe.wait_ge(S["proj_out"], PB * n + k + 1)
                for c in range(KC):
                    last = te.matmul(pj[k % 2][:, :], xt[:, c, :], wrel[:, c, 2 * k:2 * k + 2, :].rearrange("p r o -> p (r o)"),
                                     start=c == 0, stop=c == KC - 1)
                last.then_inc(S["proj_done"], 1)

            pe.wait_ge(S["wf_in"], KC * 16)
            with pe.Fori(0, NB) as i:
                pe.wait_ge(S["xt_ready"], i + 1)
                turn_block(i)
                pe.wait_ge(S["xt_ready"], i + 2)
                for k in range(PB):
                    project_bank(i, k)
            for d in range(2):
                pe.wait_ge(S["sorted_ready"], d + 1)
                for q in range(4):
                    if d:
                        pe.wait_ge(S["keys_copied"], q + 1)
                    for c in range(4):
                        at = (4 * q + c) * P
                        last = te.transpose(bank[q][:, c * P:(c + 1) * P], skeys[:, d, at:at + P], ident[:, :])
                    last.then_inc(S["keys_out"], 1)

            def sum_tile(i, t):
                half, s = t // HALF, t % HALF
                if s == 0:
                    pe.wait_ge(S["half_ready"], 2 * i + half + 1)
                pe.wait_ge(S["added"], TILES * i + t + (3 if t < 2 else 1))
                pe.wait_ge(gathered[s], 32 * i + 16 * half + 16)
                te.matmul(ring[t % 4][:, 0:D + 1], onehot[:, half, s, :], grow[:, s, :], start=True, stop=True).then_inc(S["mm_done"], 1)

            pe.wait_ge(S["wb_in"], KC * 16)
            pe.wait_ge(S["loop_in"], KC * 16)
            with pe.Fori(0, NB) as i:
                pe.wait_ge(S["xt_ready"], i + NB + 1)
                turn_block(i + NB)
                for t in range(2):
                    sum_tile(i, t)
                pe.wait_ge(S["xt_ready"], i + NB + 2)
                pe.wait_ge(S["h_ready"], 2 * i + 1)
                for c in range(KC):
                    last = te.matmul(ps_s[:, 0:D], xt[:, c, :], loop_sb[:, c, :], start=c == 0, stop=c == KC - 1)
                last.then_inc(S["self_done"], 1)
                for k in range(PB):
                    project_bank(i + NB, k)
                    for t in range(2 + 4 * k, 2 + 4 * k + 4):
                        sum_tile(i, t)
            with pe.Fori(PASSES, 2 * PASSES) as i:
                for t in range(TILES):
                    sum_tile(i, t)
            with pe.Fori(0, NB) as i:
                pe.wait_ge(S["xt2_ready"], i + 1)
                turn_block(i + 2 * NB)
                pe.wait_ge(S["xt2_ready"], i + 2)
                for c in range(KC):
                    last = te.matmul(ps_s[:, bass.ds(i, 1)], xt[:, c, :], wr_sb[:, c:c + 1],
                                     start=c == 0, stop=c == KC - 1)
                last.then_inc(S["wt_done"], 1)
            for n in range(8):
                pe.wait_ge(S["wt_ready"], n + 1)
                te.matmul(ps_t[:, 0:WAYS], ones[:, :], cnt_f[:, 1, :], start=True, stop=True).then_inc(S["cnt_done"], 1)
            pe.wait_ge(S["wt_ready"], 9)
            te.matmul(ps_t[:, 0:2 * NB], ones[:, :], tie[:, 0:2, :].rearrange("p a b -> p (a b)"), start=True, stop=True)
            te.matmul(ps_t[:, 2 * NB:3 * NB], tri[:, :], tie[:, 1, :], start=True, stop=True).then_inc(S["cnt_done"], 1)

            def ffn_group(first, base, width, blocks):
                for m in range(HC):
                    if m >= 2:
                        pe.wait_ge(S["hid_ready"], base + m - 1)
                    for c in range(KC):
                        last = te.matmul(bank[m % 2][:, 0:width], w1_sb[:, c, m * P:(m + 1) * P], xt2[:, c, bass.ds(first * P, width)],
                                         start=c == 0, stop=c == KC - 1)
                    last.then_inc(S["hid_done"], 1)
                pe.wait_ge(S["hid_ready"], base + HC)
                for q in range(blocks):
                    if q == 0:
                        pe.wait_ge(S["fin_ready"], first + 1)
                    for m in range(HC):
                        last = te.matmul(bank[4 + q][:, 0:D], hid[:, m, q * P:(q + 1) * P], w2_sb[:, m, :],
                                         start=m == 0, stop=m == HC - 1)
                    last.then_inc(S["y_done"], 1)

            pe.wait_ge(S["ffn_in"], 32)
            pe.wait_ge(S["thr_done"], 1)
            with pe.Fori(0, (NB - 1) // 4) as i:
                ffn_group(4 * i, i * HC, 4 * P, 4)
            ffn_group(NB - 1, (NB - 1) // 4 * HC, P, 1)


INS = {"x": "x", "src": "src", "dst": "dst", "etype": "edge_type_16", "wf": "L0_gnn_Wf", "wb": "L0_gnn_Wb",
       "loop_w": "L0_gnn_loop_weight", "fwd_bias": "L0_gnn_forward_bias", "bwd_bias": "L0_gnn_backward_bias",
       "self_bias": "L0_gnn_self_bias", "wr": "L0_ffn_wr", "br": "L0_ffn_br", "w1": "L0_ffn_w1",
       "b1": "L0_ffn_b1", "w2": "L0_ffn_w2", "b2": "L0_ffn_b2"}


def kernel(**inputs):
    import concourse.bacc as bacc
    from concourse.bass_utils import run_bass_kernel_spmd

    nc = bacc.Bacc("TRN2", target_bir_lowering=False, num_devices=1)
    arrays, args = {}, {}
    for name, given in INS.items():
        a = np.ascontiguousarray(inputs[given])
        arrays[f"in_{name}"] = a
        args[name] = nc.dram_tensor(f"in_{name}", a.shape, mybir.dt.from_np(a.dtype), kind="ExternalInput").ap()
    n, d = inputs["x"].shape
    rels = inputs["L0_gnn_Wf"].shape[0]
    rows = -(-n // P) * P * rels
    for name in ("table_f", "table_b"):
        args[name] = nc.dram_tensor(name, (rows, d), F32).ap()
    args["out"] = nc.dram_tensor("out_0", (n, d), F32, kind="ExternalOutput").ap()
    gnn_ffn_kernel(nc, **args)
    r = run_bass_kernel_spmd(nc, [arrays], core_ids=[0])
    return np.asarray(r.results[0]["out_0"])
```

```python
from contextlib import ExitStack

import numpy as np

import concourse.bass as bass
from concourse import mybir

F32 = mybir.dt.float32
BF16 = mybir.dt.bfloat16
I32 = mybir.dt.int32
ALU = mybir.AluOpType
ACT = mybir.ActivationFunctionType
AX = mybir.AxisListType

P = 128

TOP = 0x40000000
ROW_BITS = 17
LANE_BITS = 11
LANE = 1 << LANE_BITS
TILES = 34
HALF = TILES // 2
HIST = 336
EPS = 1e-5


def bits_as_float(v):
    return float(np.array([v], np.uint32).view(np.float32)[0])


def gnn_ffn_kernel(nc, x, src, dst, etype, wf, wb, loop_w, fwd_bias, bwd_bias, self_bias,
                   wr, br, w1, b1, w2, b2, table_f, table_b, x_self, out):
    N, D = x.shape
    E = src.shape[0]
    R = wf.shape[0]
    H = w1.shape[1]
    NB = -(-N // P)
    LAST = N - (NB - 1) * P
    KC = D // P
    HC = H // P
    PAD_ROW = N * R
    EP = 125
    EC = E // EP
    PADS = P - 1
    PASSES = NB
    KEYS = 107 * 16
    K_TOP = max(1, N // 2) - 1
    assert EP * EC == E and EC + PADS <= LANE and N <= 1 << 13 and D == 256
    assert NB % 7 == 0 and NB % 4 == 1
    assert PASSES * TILES * P >= E + NB * PADS and KEYS >= (PASSES + 1) * TILES
    SENTINEL = TOP | (NB << 24) | PAD_ROW
    PB = R * D // 512
    PARTS = 21
    ROW_STAGES = LANE_BITS * (LANE_BITS + 1) // 2 + 1
    ROW_PASSES = 10
    MERGE_PASSES = 4
    SPLIT = ROW_PASSES + 7 * MERGE_PASSES
    RING = 22
    SELF_AT = 6
    TURN_AT = PB - 2
    CHUNK = 7
    EARLY = 4
    WAYS = 15

    with ExitStack() as ctx:
        def sb(name, shape, dt=F32):
            return ctx.enter_context(nc.sbuf_tensor(name, shape, dt))

        def pb(name, shape, dt=F32):
            return ctx.enter_context(nc.psum_tensor(name, shape, dt))

        def sem(name):
            return ctx.enter_context(nc.semaphore(name))

        h_mem = sb("h_mem", [P, NB * D])
        h = h_mem[:, :].rearrange("p (b d) -> p b d", d=D)
        acc_mem = sb("acc_mem", [P, NB * (D + 1)])
        acc = acc_mem[:, :].rearrange("p (b c) -> p b c", c=D + 1)
        skeys = acc_mem[:, 0:2 * LANE].rearrange("p (a f) -> p a f", a=2)
        skeys_i = skeys.bitcast(I32)
        HELD_AT = NB - 3 * LANE // D
        held = h_mem[:, HELD_AT * D:NB * D].rearrange("p (a f) -> p a f", a=3)
        assert RING % 2 == 0 and SPLIT % 2 == 0 and RING + 2 <= HELD_AT <= SPLIT + 2
        work = [acc_mem[:, (2 + a) * LANE:(3 + a) * LANE] for a in range(2)]
        work_i = [w.bitcast(I32) for w in work]
        typ_i = acc_mem[:, 4 * LANE:4 * LANE + EC].bitcast(I32)
        xt2 = acc_mem[:, 0:NB * KC * P].rearrange("p (b c n) -> p b c n", b=NB, c=KC)
        w_mem = sb("w_mem", [P, KC * R * D])
        wrel = w_mem[:, :].rearrange("p (c r o) -> p c r o", c=KC, r=R)
        w1_sb = w_mem[:, 0:KC * H].rearrange("p (c m) -> p c m", c=KC)
        w2_sb = w_mem[:, KC * H:KC * H + HC * D].rearrange("p (c o) -> p c o", c=HC)
        g_mem = sb("g_mem", [P, HALF * (D + 1)])
        grow = g_mem[:, :].rearrange("p (s c) -> p s c", c=D + 1)
        hot_hi = g_mem[:, 0:HIST * 8].bitcast(BF16).rearrange("p (a c v) -> p a c v", a=2, v=8)
        oh_mem = sb("oh_mem", [P, 2 * HALF * P])
        onehot = oh_mem[:, :].rearrange("p (a s n) -> p a s n", a=2, s=HALF)
        hot_lo = oh_mem[:, 0:HIST * 8].bitcast(BF16).rearrange("p (a c v) -> p a c v", a=2, v=8)
        hid = oh_mem[:, 0:HC * 512].rearrange("p (c n) -> p c n", c=HC)
        stage = sb("stage", [P, 2, R * D // 2])
        keys = sb("keys", [P, PASSES * TILES + KEYS], I32)
        ends_i = [keys[:, a * EC:(a + 1) * EC] for a in range(2)]
        loop_sb = sb("loop_sb", [P, KC, D])
        ident = sb("ident", [P, P])
        iota_f = sb("iota_f", [P, P])
        xh = sb("xh", [P, 2, D])
        xts = sb("xts", [P, 2, KC, P])
        bias_bc = sb("bias_bc", [P, 4, D])
        first_at = [4 * LANE + EC]

        def first(size):
            first_at[0] += size
            return acc_mem[:, first_at[0] - size:first_at[0]]

        iota_i = first(P).bitcast(I32)
        one = first(1)
        blkmask = first(P)
        sel_hi = first(64)
        sel_lo = first(64)
        hist_s = first(P)
        hist_c = first(64)
        pad_i = first(P).bitcast(I32)
        sgn3 = sb("sgn3", [P, 3, 8])
        small_i = sb("small_i", [P, 16], I32)
        sgn = sb("sgn", [P, 8])
        sgn2 = sb("sgn2", [P, 8])
        padn = sb("padn", [P, 4])
        stats = stage[:, 1, 0:NB * 6].rearrange("p (b c) -> p b c", c=6)
        mv = sb("mv", [P, NB, 2])
        mneg = sb("mneg", [P, NB])
        rstd = sb("rstd", [P, NB])
        lt = sb("lt", [P, NB])
        rows_i = sb("rows_i", [P, 2, HALF + 3], I32)
        loc_i = sb("loc_i", [P, 2, HALF + 3], I32)
        loc_f = sb("loc_f", [P, 2, HALF + 3])
        pad_f = sb("pad_f", [P, 2, HALF + 3])
        blk_i = sb("blk_i", [1, 2, HALF + 3], I32)
        late_at = [0]

        def late(*shape):
            size = int(np.prod(shape))
            at = g_mem[:, late_at[0]:late_at[0] + size]
            late_at[0] += size
            return at if len(shape) == 1 else at.rearrange("p (a b) -> p a b", a=shape[0])

        inv = sb("inv", [P, NB])
        has = sb("has", [P, NB])
        wts = late(NB)
        key_i = late(2, NB).bitcast(I32)
        key_f = late(2, NB)
        cmp_f = stage[:, 0, 0:WAYS * NB].rearrange("p (w b) -> p w b", w=WAYS)
        cnt_f = late(2, WAYS)
        steps_f = late(WAYS + 1)
        thr = sb("thr", [P, 4])
        tie = late(4, NB)
        wr_sb = sb("wr_sb", [P, KC])
        b1_sb = sb("b1_sb", [P, HC])
        br_sb = sb("br_sb", [P, 1])
        wsel = late(NB)
        y_kept = w_mem[:, KC * H + HC * D:KC * H + HC * D + EARLY * 4 * D].rearrange("p (b d) -> p b d", d=D)
        ybuf = late(2, D)
        tri = late(P)
        ones = late(P)

        bank = [pb(f"bank{n}", [P, 512]) for n in range(8)]
        ring = bank[0:4]
        pj = bank[4:6]
        ps_t = bank[6]
        ps_s = bank[7]

        names = ("x_in edges_in bias_in wf_in wb_in loop_in ffn_in const_ready dve_chain stats_ready "
                 "hot_ready hist_chunk hist_masked hist_sum hist_picked hist_total "
                 "keys_out keys_copied sorted_ready held_free stage_done xh_part xh_ready turned xt_ready "
                 "proj_done proj_out half_ready hot_parts onehots_ready mm_done added self_done h_ready "
                 "ring_out ring_in restored wt_done wt_ready cmp_ready cnt_done y_out loop_chain fin_steps hid_done hid_ready "
                 "y_done fin_ready gather_go blocks_go pool_const xt2_ready wt_mask").split()
        S = {n: sem(n) for n in names}
        stored = [sem("stored_lo"), sem("stored_hi")]
        stage_free = [sem("stage_free_lo"), sem("stage_free_hi")]
        gathered = [sem(f"gathered{n}") for n in range(HALF)]
        out_done = [sem("out_done0"), sem("out_done1")]

        block = ctx.enter_context(nc.Block())

        @block.sync
        def _(sp):
            for a in range(2):
                sp.sem_inc(stage_free[a], 1)
            sp.sem_inc(S["ring_in"], 16)
            sp.wait_ge(S["const_ready"], 1)
            sp.dma_start(h[:, 0:NB - 1, :], x[0:(NB - 1) * P, :].rearrange("(b p) d -> p b d", p=P)).then_inc(S["x_in"], 16)
            sp.dma_start(h[0:LAST, NB - 1, :], x[(NB - 1) * P:N, :]).then_inc(S["x_in"], 16)
            sp.dma_start(ends_i[0][0:EP, :], dst.rearrange("(p c) -> p c", c=EC)).then_inc(S["edges_in"], 16)
            sp.dma_start(ends_i[1][0:EP, :], src.rearrange("(p c) -> p c", c=EC)).then_inc(S["edges_in"], 16)
            for c in range(KC):
                sp.dma_start(wrel[:, c], wf[:, c * P:(c + 1) * P, :].rearrange("r p o -> p r o")).then_inc(S["wf_in"], 16)
            sp.dma_start(typ_i[0:EP, :], etype.rearrange("(p c) -> p c", c=EC)).then_inc(S["edges_in"], 16)
            for c in range(KC):
                sp.dma_start(loop_sb[:, c], loop_w[c * P:(c + 1) * P, :]).then_inc(S["loop_in"], 16)
                sp.dma_start(wr_sb[:, c:c + 1], wr[c * P:(c + 1) * P, :]).then_inc(S["bias_in"], 16)
            for n, b in enumerate((fwd_bias, bwd_bias, self_bias, b2)):
                sp.dma_start(bias_bc[:, n, :], b.rearrange("(a d) -> a d", a=1).broadcast_to([P, D])).then_inc(S["bias_in"], 16)
            sp.dma_start(b1_sb[:, :], b1.rearrange("(c p) -> p c", p=P), allow_slow_non_contiguous=True).then_inc(S["bias_in"], 16)
            sp.dma_start(br_sb[:, :], br.rearrange("(a d) -> a d", a=1).broadcast_to([P, 1])).then_inc(S["bias_in"], 16)

            def turn_ring(i, slot, following):
                at = h[:, RING + slot, :]
                sp.wait_ge(S["h_ready"], 2 * i + 3)
                sp.dma_start(x_self[bass.ds(i * P, P), :], at).then_inc(S["ring_out"], 16)
                if following:
                    sp.wait_ge(S["ring_out"], (i - RING + 1) * 16)
                    sp.dma_start(at, x[bass.ds((i + 2) * P, P), :]).then_inc(S["ring_in"], 16)

            def restore(start, stop):
                sp.dma_start(h[:, start:stop, :], x_self[start * P:stop * P, :].rearrange("(b p) d -> p b d", p=P)).then_inc(S["restored"], 16)

            def store_block(table, i, n, between=None):
                t = table.rearrange("(b p r) d -> b p (r d)", p=P, r=R)
                for a in range(2):
                    sp.wait_ge(S["proj_out"], n * PB + (a + 1) * (PB // 2) + 2)
                    sp.dma_start(t[bass.ds(i, 1), :, a * (R * D // 2):(a + 1) * (R * D // 2)].rearrange("a p f -> (a p) f"),
                                 stage[:, a, :]).then_inc(stored[a], 16)
                    sp.wait_ge(stored[a], (n + 1) * 16)
                    sp.sem_inc(stage_free[a], 1)
                    if a == 0 and between is not None:
                        between()

            with sp.Fori(0, NB) as i:
                store_block(table_f, i, i)
            sp.wait_ge(S["proj_done"], NB * PB)
            for c in range(KC):
                sp.dma_start(wrel[:, c], wb[:, c * P:(c + 1) * P, :].rearrange("r p o -> p r o")).then_inc(S["wb_in"], 16)
            with sp.Fori(0, RING) as i:
                store_block(table_b, i, i + NB)
            with sp.Fori(RING // 2, SPLIT // 2) as j:
                for a in range(2):
                    store_block(table_b, 2 * j + a, 2 * j + a + NB, lambda: turn_ring(2 * j + a, a, True))
            sp.wait_ge(S["held_free"], 1)
            sp.dma_start(h[:, SPLIT + 2:NB - 1, :], x[(SPLIT + 2) * P:(NB - 1) * P, :].rearrange("(b p) d -> p b d", p=P)).then_inc(S["x_in"], 16)
            sp.dma_start(h[0:LAST, NB - 1, :], x[(NB - 1) * P:N, :]).then_inc(S["x_in"], 16)
            restore(RING + 2, SPLIT)
            for a in range(2):
                store_block(table_b, SPLIT + a, SPLIT + a + NB, lambda: turn_ring(SPLIT + a, a, False))
            sp.wait_ge(S["ring_out"], (SPLIT + 2 - RING) * 16)
            restore(RING, RING + 2)
            restore(SPLIT, SPLIT + 2)
            with sp.Fori(SPLIT + 2, NB) as i:
                store_block(table_b, i, i + NB)
            sp.wait_ge(S["proj_done"], 2 * NB * PB)
            sp.dma_start(w1_sb, w1.rearrange("(c p) m -> p c m", p=P)).then_inc(S["ffn_in"], 16)
            sp.dma_start(w2_sb, w2.rearrange("(c p) o -> p c o", p=P)).then_inc(S["ffn_in"], 16)
            with sp.Fori(0, (NB - 1) // 2) as i:
                for a in range(2):
                    sp.wait_ge(S["fin_ready"], 2 * i + a + 2)
                    sp.dma_start(out[bass.ds(i * 2 * P + a * P, P), :], h[:, bass.ds(2 * i + a, 1), :].rearrange("p a d -> p (a d)")).then_inc(out_done[a], 16)
            sp.wait_ge(S["fin_ready"], NB + 1)
            sp.dma_start(out[(NB - 1) * P:N, :], h[0:LAST, NB - 1, :]).then_inc(out_done[0], 16)
            sp.wait_ge(out_done[0], ((NB - 1) // 2 + 1) * 16)
            sp.wait_ge(out_done[1], ((NB - 1) // 2) * 16)

        @block.gpsimd
        def _(pool):
            g = nc.gpsimd
            g.memset(h[:, NB - 1, :], 0.0).then_inc(S["const_ready"], 1)
            g.iota(iota_i[:, :], pattern=[[1, P]], base=0, channel_multiplier=0).then_inc(S["pool_const"], 1)
            g.iota(small_i[:, 0:8], pattern=[[0, 8]], base=0, channel_multiplier=1).then_inc(S["pool_const"], 1)
            g.iota(pad_i[:, :], pattern=[[1, P]], base=PAD_ROW, channel_multiplier=0).then_inc(S["pool_const"], 1)
            g.memset(ident[:, :], 0.0).then_inc(S["pool_const"], 1)
            g.memset(one, 1.0).then_inc(S["pool_const"], 1)
            pool.wait_ge(S["pool_const"], 5)
            g.affine_select(out=ident[:, :], in_=ident[:, :], compare_op=ALU.not_equal, fill=1.0,
                            base=0, pattern=[[-1, P]], channel_multiplier=1).then_inc(S["pool_const"], 1)
            for hot in (hot_hi, hot_lo):
                for a in range(2):
                    g.memset(hot[:, a, HIST - 6:HIST, :], 0.0).then_inc(S["pool_const"], 1)
            pool.wait_ge(S["hist_chunk"], 2 * (EC // (HIST - 6)))
            g.memset(grow[:, :, D:D + 1], 1.0).then_inc(S["pool_const"], 1)

            def gather(table, i):
                for t in range(TILES):
                    half, s = t // HALF, t % HALF
                    pool.wait_ge(S["mm_done"], TILES * i + t + 1)
                    if s == 0:
                        pool.wait_ge(S["half_ready"], 2 * i + half + 1)
                    pool.sem_inc(S["gather_go"], 1)
                    g.indirect_dma_start(grow[:, s, 0:D], None, table,
                                         bass.IndirectOffsetOnAxis(rows_i[:, half, s:s + 1], 0)).then_inc(gathered[s], 16)

            pool.wait_ge(S["pool_const"], 11)
            for a in range(2):
                pool.wait_ge(stored[a], NB * 16)
            with pool.Fori(0, PASSES) as i:
                gather(table_f, i)
            for a in range(2):
                pool.wait_ge(stored[a], 2 * NB * 16)
            with pool.Fori(PASSES, 2 * PASSES) as i:
                gather(table_b, i)
            pool.wait_ge(S["mm_done"], 2 * PASSES * TILES + HALF)
            g.memset(ones[:, :], 1.0).then_inc(S["pool_const"], 1)
            pool.wait_ge(S["pool_const"], 12)
            g.affine_select(out=tri[:, :], in_=ones[:, :], compare_op=ALU.is_gt, fill=0.0,
                            base=0, pattern=[[1, P]], channel_multiplier=-1).then_inc(S["pool_const"], 1)

        @block.scalar
        def _(act):
            a_ = nc.scalar
            act.sem_inc(S["proj_out"], 2)
            act.sem_inc(S["xt_ready"], 1)
            act.sem_inc(S["xt2_ready"], 1)
            act.wait_ge(S["stats_ready"], 1)

            def norm_block(i, n, at=None):
                act.wait_ge(S["turned"], n + 1)
                a_.activation(xh[:, 0, :], h[:, bass.ds(i if at is None else at, 1), :].rearrange("p a d -> p (a d)"), ACT.Identity,
                              bias=mneg[:, bass.ds(i, 1)]).then_inc(S["xh_part"], 1)
                act.wait_ge(S["xh_part"], n + 1)
                a_.activation(xh[:, 1, :], xh[:, 0, :], ACT.Copy, scale=rstd[:, bass.ds(i, 1)]).then_inc(S["xh_ready"], 1)

            def copy_turned(n, odd):
                act.wait_ge(S["turned"], n + 2)
                a_.activation(xts[:, odd, :, :].rearrange("p c n -> p (c n)"), ps_t[:, odd * KC * P:(odd + 1) * KC * P],
                              ACT.Copy).then_inc(S["xt_ready"], 1)

            def one_hots(i, half):
                act.wait_ge(S["half_ready"], 2 * i + half + 1)
                for s in range(HALF):
                    a_.activation(onehot[:, half, s, :], iota_f[:, :], ACT.Abs, bias=loc_f[:, half, s:s + 1]).then_inc(S["hot_parts"], 1)
                act.wait_ge(S["hot_parts"], (2 * i + half + 1) * HALF)
                both = onehot[:, half, :, :].rearrange("p s n -> p (s n)")
                a_.activation(both, both, ACT.Relu, scale=-1.0, bias=1.0).then_inc(S["onehots_ready"], 1)

            def project_out(n, following, odd, i=None, at=None):
                if following is not None:
                    norm_block(following, n + 1, at)
                for k in range(PB):
                    half, at = k // (PB // 2), k % (PB // 2) * 512
                    if k == TURN_AT and following is not None:
                        copy_turned(n + 1, 1 - odd)
                    act.wait_ge(S["proj_done"], n * PB + k + 1)
                    if at == 0:
                        act.wait_ge(stage_free[half], n + 1)
                    a_.activation(stage[:, half, at:at + 512], pj[k % 2][:, :], ACT.Copy).then_inc(S["proj_out"], 1)
                    if i is not None and k == 4:
                        one_hots(i + 1, 0)
                if i is not None:
                    one_hots(i + 1, 1)

            def project_pairs(start, stop, base):
                with act.Fori(start // 2, stop // 2) as j:
                    for a in range(2):
                        project_out(2 * j + a + base, 2 * j + a + 1, (a + base) % 2, 2 * j + a if base else None)

            norm_block(0, 0)
            copy_turned(0, 0)
            project_pairs(0, NB - 1, 0)
            project_out(NB - 1, 0, (NB - 1) % 2)
            for half in range(2):
                one_hots(0, half)
            project_pairs(0, RING, NB)

            def project_ring(i, a):
                act.wait_ge(S["ring_in"], (i + 1 - RING) * 16)
                project_out(i + NB, i + 1, (a + NB) % 2, i, RING + 1 - a)

            with act.Fori(RING // 2, SPLIT // 2) as j:
                for a in range(2):
                    project_ring(2 * j + a, a)
            project_ring(SPLIT, 0)
            act.wait_ge(S["x_in"], 64)
            project_out(SPLIT + 1 + NB, SPLIT + 2, (1 + NB) % 2, SPLIT + 1)
            project_pairs(SPLIT + 2, NB - 1, NB)
            project_out(2 * NB - 1, None, (2 * NB - 1) % 2, NB - 1)
            with act.Fori(PASSES, 2 * PASSES - 1) as i:
                for half in range(2):
                    one_hots(i + 1, half)
            def norm_chunk(c):
                act.wait_ge(S["stats_ready"], c + 2)
                with act.Fori(CHUNK * c, CHUNK * (c + 1)) as i:
                    norm_block(i, i + 2 * NB)
                    act.wait_ge(S["turned"], i + 2 * NB + 2)
                    a_.activation(xts[:, 0, :, :].rearrange("p c n -> p (c n)"), ps_t[:, 0:KC * P], ACT.Copy).then_inc(S["xt_ready"], 1)
                    a_.activation(xt2[:, bass.ds(i, 1)].rearrange("p a c n -> p (a c n)"), ps_t[:, 0:KC * P],
                                  ACT.Copy).then_inc(S["xt2_ready"], 1)

            def hidden(g, width):
                for m in range(HC):
                    act.wait_ge(S["hid_done"], g * HC + m + 1)
                    a_.activation(hid[:, m, 0:width], bank[m % 2][:, 0:width], ACT.Gelu_apprx_tanh,
                                  bias=b1_sb[:, m:m + 1]).then_inc(S["hid_ready"], 1)

            def keep(g):
                for q in range(4):
                    act.wait_ge(S["y_done"], 4 * g + q + 1)
                    a_.activation(y_kept[:, 4 * g + q, :], bank[2 + q][:, 0:D], ACT.Copy).then_inc(S["y_out"], 1)

            norm_chunk(0)
            act.wait_ge(S["ffn_in"], 32)
            for g in range(EARLY):
                hidden(g, 4 * P)
                keep(g)
                for c in range(2 * g + 1, min(2 * g + 3, NB // CHUNK)):
                    norm_chunk(c)
            with act.Fori(EARLY, NB // 4) as g:
                act.wait_ge(S["y_done"], 4 * g)
                hidden(g, 4 * P)
            act.wait_ge(S["y_done"], NB - 1)
            hidden(NB // 4, P)

        @block.vector
        def _(dve):
            v = nc.vector
            links = [0]
            for name in ("h_ready", "fin_ready"):
                dve.sem_inc(S[name], 1)

            def link(*ins):
                for x_ in ins:
                    links[0] += 1
                    x_.then_inc(S["dve_chain"], 1)
                dve.wait_ge(S["dve_chain"], links[0])

            dve.wait_ge(S["pool_const"], 10)
            link(v.memset(skeys[:, :, :], bits_as_float(SENTINEL)),
                 v.tensor_copy(iota_f[:, :], iota_i[:, :]))

            def statistics(b):
                return v.bn_stats(stats[:, b, :], h[:, b, :])

            local = [0]

            def step(*ins):
                for x_ in ins:
                    local[0] += 1
                    x_.then_inc(S["loop_chain"], 1)
                dve.wait_ge(S["loop_chain"], local[0])

            def end_steps():
                local[0] = 0
                dve.sem_clear(S["loop_chain"])

            def finish_statistics(mean, var, neg, inv_std, t):
                step(v.tensor_scalar(neg, mean, -1.0, None, ALU.mult),
                     v.tensor_scalar(var, var, 1.0, EPS, ALU.mult, ALU.add))
                step(v.tensor_scalar(t.bitcast(I32), var.bitcast(I32), 1, None, ALU.logical_shift_right))
                step(v.tensor_scalar(inv_std.bitcast(I32), t.bitcast(I32), -1.0, float(0x5F3759DF), ALU.mult, ALU.add))
                for _ in range(3):
                    step(v.tensor_tensor(t, inv_std, inv_std, ALU.mult))
                    step(v.tensor_tensor(t, t, var, ALU.mult))
                    step(v.tensor_scalar(t, t, -0.5, 1.5, ALU.mult, ALU.add))
                    step(v.tensor_tensor(inv_std, inv_std, t, ALU.mult))

            dve.wait_ge(S["x_in"], 32)
            link(*[statistics(b) for b in range(NB)])
            link(*[v.bn_aggr(mv[:, b, :], stats[:, b, :]) for b in range(NB)])
            link(v.tensor_copy(inv[:, :], mv[:, :, 1]))
            finish_statistics(mv[:, :, 0], inv[:, :], mneg[:, :], rstd[:, :], lt[:, :])
            end_steps()
            v.tensor_copy(padn[:, 3:4], iota_f[:, 0:1]).then_inc(S["stats_ready"], 1)

            link(*[v.tensor_scalar(small_i[:, 8 + b:9 + b], small_i[:, b:b + 1], b, 1,
                                   ALU.logical_shift_right, ALU.bitwise_and) for b in range(7)])
            link(v.tensor_scalar(sgn[:, 0:7], small_i[:, 8:15], -2.0, 1.0, ALU.mult, ALU.add))
            link(v.tensor_tensor(sgn2[:, 1:7], sgn[:, 0:6], sgn[:, 1:7], ALU.mult))
            link(v.tensor_scalar(hist_s[:, :].bitcast(I32), iota_i[:, :], 3, None, ALU.logical_shift_right),
                 v.tensor_scalar(small_i[:, 8:9], small_i[:, 0:1], 3, None, ALU.logical_shift_right),
                 v.tensor_scalar(small_i[:, 9:10], small_i[:, 0:1], 7, None, ALU.bitwise_and),
                 v.tensor_scalar(hist_c[:, :].bitcast(I32), iota_i[:, 0:64], 7, None, ALU.bitwise_and))
            link(v.tensor_copy(padn[:, 0:2], small_i[:, 8:10]),
                 v.tensor_copy(iota_f[:, :], hist_s[:, :].bitcast(I32)),
                 v.tensor_copy(sel_lo, hist_c[:, :].bitcast(I32)))
            link(v.tensor_scalar(blkmask, iota_f[:, :], padn[:, 0:1], None, ALU.is_equal),
                 v.tensor_scalar(sel_hi, iota_f[:, 0:64], padn[:, 1:2], None, ALU.is_equal),
                 v.tensor_scalar(sel_lo, sel_lo, padn[:, 1:2], None, ALU.is_equal))
            link(v.tensor_copy(iota_f[:, :], iota_i[:, :]))

            dve.wait_ge(S["edges_in"], 48)
            W = HIST - 6
            for d in range(2):
                node = ends_i[d][0:EP, :]
                link(v.tensor_scalar(work_i[0][0:EP, 0:EC], node, 10, None, ALU.logical_shift_right),
                     v.tensor_scalar(work_i[1][0:EP, 0:EC], node, 7, 7, ALU.logical_shift_right, ALU.bitwise_and))
                for c in range(EC // W):
                    n = d * (EC // W) + c
                    if n >= 2:
                        dve.wait_ge(S["hist_chunk"], n - 1)
                    for digit, hot in ((0, hot_hi), (1, hot_lo)):
                        v.tensor_tensor(hot[0:EP, n % 2, 0:W, :],
                                        work_i[digit][0:EP, c * W:(c + 1) * W].unsqueeze(2).broadcast_to([EP, W, 8]),
                                        iota_f[0:EP, 0:8].unsqueeze(1).broadcast_to([EP, W, 8]),
                                        ALU.is_equal).then_inc(S["hot_ready"], 1)
                dve.wait_ge(S["hot_ready"], 2 * (d + 1) * (EC // W))
            for d in range(2):
                dve.wait_ge(S["hist_chunk"], 2 * (EC // W))
                v.tensor_tensor(hist_s[:, :], bank[d][:, 0:P], blkmask, ALU.mult).then_inc(S["hist_masked"], 1)
                dve.wait_ge(S["hist_sum"], d + 1)
                v.tensor_tensor(hist_c[:, :], bank[2][:, 0:64], sel_lo, ALU.mult).then_inc(S["hist_picked"], 1)
                dve.wait_ge(S["hist_total"], d + 1)
                link(v.tensor_scalar(small_i[0:64, 8:9], bank[3][0:64, 0:1], -1.0, None, ALU.mult))
                link(v.tensor_scalar(small_i[0:64, 9:10], small_i[0:64, 8:9], P - 1, None, ALU.bitwise_and))
                link(v.tensor_copy(padn[0:64, 0:1], small_i[0:64, 9:10]))
                link(v.tensor_scalar(small_i[0:64, 10:11], small_i[0:64, 0:1], 24, TOP, ALU.logical_shift_left, ALU.bitwise_or))
                link(v.tensor_tensor(hist_s[0:64, :].bitcast(I32), pad_i[0:64, :],
                                     small_i[0:64, 10:11].broadcast_to([64, P]), ALU.bitwise_or),
                     v.tensor_scalar(work[0][0:64, 0:P], iota_f[0:64, :], padn[0:64, 0:1], None, ALU.is_lt))
                link(v.copy_predicated(skeys[0:NB, d, EC:EC + PADS], work_i[0][0:NB, 0:PADS],
                                       hist_s[0:NB, 0:PADS]))
                link(v.tensor_scalar(work_i[0][0:EP, 0:EC], ends_i[d][0:EP, :], ROW_BITS, TOP,
                                     ALU.logical_shift_left, ALU.bitwise_or),
                     v.tensor_scalar(work_i[1][0:EP, 0:EC], ends_i[1 - d][0:EP, :], 4, None, ALU.logical_shift_left))
                link(v.tensor_tensor(work_i[0][0:EP, 0:EC], work_i[0][0:EP, 0:EC], work_i[1][0:EP, 0:EC], ALU.bitwise_or))
                link(v.tensor_tensor(skeys_i[0:EP, d, 0:EC], work_i[0][0:EP, 0:EC], typ_i[0:EP, :], ALU.bitwise_or))

            link(v.memset(sgn3[:, :, :], 1.0))
            link(v.tensor_copy(sgn3[:, 0, 0:5], sgn2[:, 1:6]),
                 v.tensor_copy(sgn3[:, 0, 5:6], sgn[:, 6:7]),
                 v.tensor_copy(sgn3[:, 1, 6:7], sgn2[:, 6:7]),
                 v.tensor_copy(sgn3[:, 2, 5:6], sgn[:, 5:6]),
                 v.tensor_copy(sgn3[:, 2, 6:7], sgn[:, 5:6]))
            done = S["stage_done"]
            cur, count, bufs, flips = None, 0, work, 0

            def other():
                nonlocal flips
                flips += 1
                return bufs[flips % 2]

            def put(ins):
                nonlocal count
                count += 1
                ins.then_inc(done, 1)

            def ready():
                if count:
                    dve.wait_ge(done, count)

            def directed_half(m, k, r, to):
                a, b = (y.rearrange("p (g r h t l) -> p g r h t l", r=2, h=1 << (m - 1 - k), t=2, l=1 << k)
                        for y in (cur, to))
                put(v.tensor_tensor(b[:, :, r, :, r, :], a[:, :, r, :, 0, :], a[:, :, r, :, 1, :], ALU.min))
                put(v.tensor_tensor(b[:, :, r, :, 1 - r, :], a[:, :, r, :, 0, :], a[:, :, r, :, 1, :], ALU.max))

            def ascend_half(k, which, to):
                a, b = (y.rearrange("p (h t l) -> p h t l", t=2, l=1 << k) for y in (cur, to))
                put(v.tensor_tensor(b[:, :, which, :], a[:, :, 0, :], a[:, :, 1, :], (ALU.min, ALU.max)[which]))

            def ascend(k, to=None):
                nonlocal cur
                ready()
                to = other() if to is None else to
                for which in range(2):
                    ascend_half(k, which, to)
                cur = to

            def negate(sign):
                nonlocal cur
                ready()
                to = other()
                put(v.tensor_scalar(to, cur, sign, None, ALU.mult))
                cur = to

            def turn():
                nonlocal cur
                ready()
                to = other()
                put(v.transpose(to, cur))
                cur = to

            def quadrants(bit):
                nonlocal cur
                ready()
                to = other()
                for q in range(4):
                    w = q ^ bit
                    put(v.tensor_scalar(to[32 * q:32 * q + 32], cur[32 * w:32 * w + 32], -1.0, None, ALU.mult))
                ready()
                put(v.tensor_tensor(to, cur, to, ALU.min))
                cur = to

            row_stages = [(m, k) for m in range(1, LANE_BITS) for k in reversed(range(m))] + [None]
            row_stages += [(LANE_BITS, k) for k in reversed(range(LANE_BITS))]
            assert len(row_stages) == ROW_STAGES

            def row_half(n, lanes):
                nonlocal cur, count
                stage_n, half = n // 2, n % 2
                if n == 0:
                    cur, count = lanes, 0
                if row_stages[stage_n] is None:
                    if half == 0:
                        negate(sgn[:, 0:1])
                    return
                m, k = row_stages[stage_n]
                final = stage_n == ROW_STAGES - 1
                if half == 0:
                    ready()
                    other()
                to = lanes if final else bufs[flips % 2]
                if m < LANE_BITS:
                    directed_half(m, k, half, to)
                else:
                    ascend_half(k, half, to)
                if half == 1:
                    cur = to
                    if final:
                        ready()
                        dve.sem_clear(done)

            def only_from(c, least, step):
                nonlocal cur, count, flips
                ready()
                was = cur, count, flips
                with dve.If(c >= least):
                    step()
                now = cur, count, flips
                with dve.Else():
                    if now[2] % 2 != was[2] % 2:
                        v.tensor_copy(now[0], was[0]).then_inc(done, now[1] - was[1])
                    else:
                        dve.sem_inc(done, now[1] - was[1])

            def merge_half(c, part, half, lanes):
                nonlocal cur, count
                plain = part in range(8, 15) or part > 15
                if plain:
                    k = 0 if part == 8 else LANE_BITS + 8 - part if part < 15 else 20 - part
                    if half == 0:
                        ready()
                        ascend_half(k, 0, lanes if part == 20 else other())
                    else:
                        to = lanes if part == 20 else bufs[flips % 2]
                        ascend_half(k, 1, to)
                        cur = to
                    if part == 20 and half == 1:
                        ready()
                        dve.sem_clear(done)
                elif half == 1:
                    return
                elif part == 0:
                    cur, count = lanes, 0
                    negate(sgn3[:, 0, bass.ds(c, 1)])
                elif part == 1:
                    only_from(c, 6, lambda: (quadrants(2), negate(sgn3[:, 1, bass.ds(c, 1)])))
                elif part == 2:
                    only_from(c, 5, lambda: (quadrants(1), negate(sgn3[:, 2, bass.ds(c, 1)])))
                elif part in (3, 15):
                    turn()
                else:
                    only_from(c, 8 - part, lambda: ascend(8 - part))

            for n in range(2 * ROW_STAGES):
                row_half(n, skeys[:, 0, :])
            with dve.Fori(0, 7) as c:
                for part in range(PARTS):
                    for half in range(2):
                        merge_half(c, part, half, skeys[:, 0, :])
            v.tensor_copy(small_i[:, 8:9], small_i[:, 0:1]).then_inc(S["sorted_ready"], 1)
            def copy_keys(d, q, source):
                dve.wait_ge(S["keys_out"], 4 * d + q + 1)
                to = keys[:, d * PASSES * TILES:d * PASSES * TILES + KEYS].rearrange("p (r c) -> p c r", c=16)
                v.tensor_copy(to[:, 4 * q:4 * q + 4, :],
                              source[:, :].bitcast(I32).rearrange("p (c r) -> p c r", c=4)[:, :, 0:KEYS // 16]).then_inc(S["keys_copied"], 1)

            for q in range(4):
                copy_keys(0, q, bank[q])
            dve.wait_ge(S["keys_copied"], 4)

            def stage_half(i, half, wait):
                kt = keys[:, bass.ds(i * TILES + half * HALF, HALF)]
                v.tensor_scalar(rows_i[:, half, 0:HALF], kt, (1 << ROW_BITS) - 1, None, ALU.bitwise_and).then_inc(S["cmp_ready"], 1)
                v.tensor_scalar(loc_i[:, half, 0:HALF], kt, ROW_BITS, P - 1, ALU.logical_shift_right, ALU.bitwise_and).then_inc(S["cmp_ready"], 1)
                v.tensor_scalar(blk_i[0:1, half, 0:HALF], kt[0:1, :], 24, 63,
                                ALU.logical_shift_right, ALU.bitwise_and).then_inc(S["cmp_ready"], 1)
                dve.wait_ge(S["cmp_ready"], wait + 3)
                v.tensor_scalar(pad_f[:, half, 0:HALF], rows_i[:, half, 0:HALF], float(PAD_ROW), -1000.0,
                                ALU.is_ge, ALU.mult).then_inc(S["cmp_ready"], 1)
                v.tensor_scalar(blk_i[0:1, half, 0:HALF], blk_i[0:1, half, 0:HALF], float(NB - 1), None, ALU.min).then_inc(S["cmp_ready"], 1)
                dve.wait_ge(S["cmp_ready"], wait + 5)
                v.tensor_tensor(loc_f[:, half, 0:HALF], pad_f[:, half, 0:HALF], loc_i[:, half, 0:HALF], ALU.subtract).then_inc(S["half_ready"], 1)

            for half in range(2):
                stage_half(0, half, 5 * half)
            dve.wait_ge(S["turned"], NB + 2)
            link(v.tensor_copy(held[:, 0, :], skeys[:, 1, :]))
            link(v.memset(acc_mem[:, :], 0.0))
            dve.sem_inc(S["added"], 4)

            def load_blocks(i, half):
                dve.wait_ge(S["half_ready"], 2 * i + half + 1)
                dve.sem_inc(S["blocks_go"], 1)
                _, blocks = nc.values_load_multi_w_load_instructions(
                    blk_i[0:1, half, 0:HALF], engines=(mybir.EngineType.DVE,), min_val=0, max_val=NB - 1,
                    skip_runtime_bounds_check_because="the block is masked to six bits and clamped to the last one")
                return blocks

            def add_tile(i, t, blk):
                dve.wait_ge(S["mm_done"], TILES * i + t + HALF + 1)
                dve.wait_ge(S["added"], TILES * i + t + 4)
                to = acc[:, bass.ds(blk, 1), :].rearrange("p a c -> p (a c)")
                v.tensor_tensor(to, ring[t % 4][:, 0:D + 1], to, ALU.add).then_inc(S["added"], 1)

            def self_loop(i, at):
                hb = h[:, bass.ds(at, 1), :].rearrange("p a d -> p (a d)")
                dve.wait_ge(S["self_done"], i + 1)
                v.scalar_tensor_tensor(out=hb, in0=ps_s[:, 0:D], scalar=2.0, in1=hb, op0=ALU.mult, op1=ALU.add).then_inc(S["h_ready"], 1)
                dve.wait_ge(S["h_ready"], 2 * i + 2)
                v.tensor_tensor(hb, hb, bias_bc[:, 2, :], ALU.add).then_inc(S["h_ready"], 1)

            def add_tiles(i, between=None, at=None):
                for half in range(2):
                    blocks = load_blocks(i, half)
                    for s in range(HALF):
                        t = half * HALF + s
                        add_tile(i, t, blocks[s])
                        if between is not None:
                            between(t)
                        if t == SELF_AT and at is not None:
                            self_loop(i, at)
                    stage_half(i + 1, half, 10 * (i + 1) + 5 * half)

            dve.wait_ge(S["bias_in"], (KC + 6) * 16)
            bufs = [held[:, 1, :], held[:, 2, :]]
            for i in range(ROW_PASSES):
                def sort_rows(t):
                    n = i * 14 + t // 2
                    if t % 2 == 1 and t < 28 and n < 2 * ROW_STAGES:
                        row_half(n, held[:, 0, :])

                add_tiles(i, sort_rows, i)

            def merge_passes(start, stop, ringed):
                with dve.Fori(start, stop) as c:
                    for a in range(MERGE_PASSES):
                        def merge(t):
                            n = 11 * a + t // 3
                            if t % 3 == 1 and n < 2 * PARTS:
                                merge_half(c, n // 2, n % 2, held[:, 0, :])

                        i = ROW_PASSES + MERGE_PASSES * c + a
                        add_tiles(i, merge, RING + a % 2 if ringed else i)

            merge_passes(0, (RING - ROW_PASSES) // MERGE_PASSES, False)
            merge_passes((RING - ROW_PASSES) // MERGE_PASSES, 7, True)
            v.tensor_copy(small_i[:, 8:9], small_i[:, 0:1]).then_inc(S["sorted_ready"], 1)
            for q in range(4):
                copy_keys(1, q, ps_t)
            dve.wait_ge(S["keys_copied"], 8)
            v.memset(h[:, NB - 1, :], 0.0).then_inc(S["held_free"], 1)
            for a in range(2):
                add_tiles(SPLIT + a, None, RING + a)
            with dve.Fori(SPLIT + 2, PASSES) as i:
                add_tiles(i, None, i)

            def fold_scales(d):
                dve.wait_ge(S["added"], (d + 1) * PASSES * TILES + 4)
                dve.wait_ge(S["h_ready"], 2 * NB + 1)
                link(v.tensor_scalar(inv[:, :], acc[:, :, D], 1.0, None, ALU.max),
                     v.tensor_scalar(has[:, :], acc[:, :, D], 1.0, None, ALU.min))
                link(v.reciprocal(inv[:, :], inv[:, :]))
                link(v.tensor_tensor(inv[:, :], inv[:, :], has[:, :], ALU.mult))

            def fold_chunk(d, c):
                rows = [h[:, bass.ds(c * CHUNK + b, 1), :].rearrange("p a d -> p (a d)") for b in range(CHUNK)]
                step(*[v.scalar_tensor_tensor(
                    out=rows[b], in0=acc[:, bass.ds(c * CHUNK + b, 1), 0:D].rearrange("p a d -> p (a d)"),
                    scalar=inv[:, bass.ds(c * CHUNK + b, 1)], in1=rows[b], op0=ALU.mult, op1=ALU.add) for b in range(CHUNK)])
                step(*[v.scalar_tensor_tensor(
                    out=rows[b], in0=bias_bc[:, d, :], scalar=has[:, bass.ds(c * CHUNK + b, 1)],
                    in1=rows[b], op0=ALU.mult, op1=ALU.add) for b in range(CHUNK)])
                return rows

            dve.wait_ge(S["restored"], 3 * 16)
            fold_scales(0)
            with dve.Fori(0, NB // CHUNK) as c:
                fold_chunk(0, c)
                end_steps()
            link(v.memset(acc_mem[:, :], 0.0))
            with dve.Fori(PASSES, 2 * PASSES) as i:
                add_tiles(i)

            fold_scales(1)
            with dve.Fori(0, NB // CHUNK) as c:
                rows = fold_chunk(1, c)
                step(*[v.bn_stats(stats[:, b, :], rows[b]) for b in range(CHUNK)])
                step(*[v.bn_aggr(mv[:, b, :], stats[:, b, :]) for b in range(CHUNK)])
                step(v.tensor_copy(lt[:, 0:CHUNK], mv[:, 0:CHUNK, 1]))
                finish_statistics(mv[:, 0:CHUNK, 0], lt[:, 0:CHUNK], mneg[:, bass.ds(c * CHUNK, CHUNK)],
                                  rstd[:, bass.ds(c * CHUNK, CHUNK)], lt[:, CHUNK:2 * CHUNK])
                end_steps()
                v.tensor_copy(padn[:, 3:4], iota_f[:, 0:1]).then_inc(S["stats_ready"], 1)

            dve.wait_ge(S["wt_done"], NB)
            link(v.tensor_scalar(wts[:, :], ps_s[:, 0:NB], br_sb[:, 0:1], None, ALU.add))
            link(v.tensor_scalar(wts[:, :], wts[:, :], 0.0, None, ALU.add))
            wt_i = wts[:, :].bitcast(I32)
            link(v.tensor_scalar(key_i[:, 0, :], wt_i, 31, None, ALU.arith_shift_right))
            link(v.tensor_scalar(key_i[:, 0, :], key_i[:, 0, :], -(1 << 31), None, ALU.bitwise_or))
            link(v.tensor_tensor(key_i[:, 0, :], key_i[:, 0, :], wt_i, ALU.bitwise_xor))
            link(v.tensor_scalar(key_i[:, 1, :], key_i[:, 0, :], 0xFFFF, None, ALU.bitwise_and))
            link(v.tensor_scalar(key_i[:, 0, :], key_i[:, 0, :], 16, 0xFFFF, ALU.logical_shift_right, ALU.bitwise_and))
            link(v.tensor_copy(key_f[:, :, :], key_i[:, :, :]))
            link(v.tensor_scalar(key_f[:, 0, NB - 1:NB], key_f[:, 0, NB - 1:NB], 1.0, None, ALU.add))
            link(v.tensor_scalar(thr[:, 2:3], small_i[:, 0:1], float(LAST), None, ALU.is_lt))
            link(v.tensor_scalar(key_f[:, 0, NB - 1:NB], key_f[:, 0, NB - 1:NB], thr[:, 2:3], -1.0, ALU.mult, ALU.add))
            link(v.tensor_scalar(steps_f[:, 0:WAYS], iota_f[:, 1:WAYS + 1], 1.0, None, ALU.mult))
            rounds = 0
            for phase in range(2):
                if phase == 1:
                    link(v.tensor_scalar(tie[:, 0, :], key_f[:, 0, :], thr[:, 0:1], None, ALU.is_equal),
                         v.tensor_scalar(tie[:, 1, :], key_f[:, 0, :], thr[:, 0:1], 65537.0, ALU.is_gt, ALU.mult),
                         v.tensor_scalar(tie[:, 2, :], key_f[:, 1, :], 1.0, None, ALU.add))
                    link(v.tensor_tensor(tie[:, 0, :], tie[:, 0, :], tie[:, 2, :], ALU.mult))
                    link(v.tensor_tensor(tie[:, 0, :], tie[:, 0, :], tie[:, 1, :], ALU.add))
                    link(v.tensor_scalar(key_f[:, 0, :], tie[:, 0, :], -1.0, None, ALU.add))
                link(v.memset(thr[:, 0:1], 0.0))
                for step in (4096.0, 256.0, 16.0, 1.0):
                    link(v.tensor_scalar(cnt_f[:, 0, :], steps_f[:, 0:WAYS], step, thr[:, 0:1], ALU.mult, ALU.add))
                    link(v.tensor_tensor(cmp_f, key_f[:, 0, :].unsqueeze(1).broadcast_to([P, WAYS, NB]),
                                         cnt_f[:, 0, :].unsqueeze(2).broadcast_to([P, WAYS, NB]), ALU.is_ge))
                    v.tensor_reduce(cnt_f[:, 1, :], cmp_f, AX.X, ALU.add).then_inc(S["wt_ready"], 1)
                    rounds += 1
                    dve.wait_ge(S["cnt_done"], rounds)
                    link(v.tensor_scalar(cnt_f[:, 1, :], ps_t[:, 0:WAYS], float(K_TOP), step, ALU.is_ge, ALU.mult))
                    link(v.tensor_reduce(thr[:, 1:2], cnt_f[:, 1, :], AX.X, ALU.add))
                    link(v.tensor_tensor(thr[:, 0:1], thr[:, 0:1], thr[:, 1:2], ALU.add))
            link(v.tensor_scalar(tie[:, 0, :], key_f[:, 0, :], thr[:, 0:1], None, ALU.is_gt))
            v.tensor_scalar(tie[:, 1, :], key_f[:, 0, :], thr[:, 0:1], None, ALU.is_equal).then_inc(S["wt_ready"], 1)
            rounds += 1
            dve.wait_ge(S["cnt_done"], rounds)
            link(v.tensor_reduce(thr[:, 1:2], ps_t[:, 0:NB], AX.X, ALU.add),
                 v.tensor_copy(tie[:, 2, :], ps_t[:, NB:2 * NB]),
                 v.memset(key_f[:, 1, :], 0.0))
            link(v.tensor_scalar(thr[:, 1:2], thr[:, 1:2], -1.0, float(K_TOP), ALU.mult, ALU.add),
                 v.tensor_tensor_scan(tie[:, 3, :], tie[:, 2, :], key_f[:, 1, :], 0.0, ALU.add, ALU.add))
            link(v.tensor_tensor(tie[:, 3, :], tie[:, 3, :], tie[:, 2, :], ALU.subtract))
            link(v.tensor_tensor(tie[:, 3, :], tie[:, 3, :], ps_t[:, 2 * NB:3 * NB], ALU.add))
            link(v.tensor_scalar(tie[:, 3, :], tie[:, 3, :], thr[:, 1:2], None, ALU.is_lt))
            link(v.tensor_tensor(tie[:, 3, :], tie[:, 3, :], tie[:, 1, :], ALU.mult))
            link(v.tensor_tensor(tie[:, 3, :], tie[:, 3, :], tie[:, 0, :], ALU.add))
            link(v.tensor_tensor(wsel[:, :], tie[:, 3, :], wts[:, :], ALU.mult))

            def finish_block(i, second):
                hb = h[:, bass.ds(i, 1), :].rearrange("p a d -> p (a d)")
                v.tensor_scalar(ybuf[:, 0, :], hb, mneg[:, bass.ds(i, 1)], rstd[:, bass.ds(i, 1)],
                                ALU.add, ALU.mult).then_inc(S["fin_steps"], 1)
                v.tensor_tensor(ybuf[:, 1, :], second, bias_bc[:, 3, :], ALU.add).then_inc(S["fin_steps"], 1)
                dve.wait_ge(S["fin_steps"], 3 * i + 1)
                v.tensor_tensor(hb, hb, ybuf[:, 0, :], ALU.add).then_inc(S["fin_steps"], 1)
                dve.wait_ge(S["fin_steps"], 3 * i + 3)
                v.scalar_tensor_tensor(out=hb, in0=ybuf[:, 1, :], scalar=wsel[:, bass.ds(i, 1)], in1=hb,
                                       op0=ALU.mult, op1=ALU.add).then_inc(S["fin_ready"], 1)
                dve.wait_ge(S["fin_ready"], i + 2)

            dve.wait_ge(S["y_out"], 4 * EARLY)
            with dve.Fori(0, 4 * EARLY) as i:
                finish_block(i, y_kept[:, bass.ds(i, 1), :].rearrange("p a d -> p (a d)"))
            with dve.Fori(EARLY, NB // 4) as g:
                for q in range(4):
                    dve.wait_ge(S["y_done"], 4 * g + q + 1)
                    finish_block(4 * g + q, bank[2 + q][:, 0:D])
            dve.wait_ge(S["y_done"], NB)
            finish_block(NB - 1, bank[2][:, 0:D])

        @block.tensor
        def _(pe):
            te = nc.tensor
            pe.sem_inc(S["mm_done"], HALF)
            pe.sem_inc(S["turned"], 1)

            def count_chunk(n):
                d, c, W = n // 5, n % 5, HIST // 16
                pe.wait_ge(S["hot_ready"], 2 * n + 2)
                for k in range(W):
                    last = te.matmul(bank[d][:, 0:P], hot_hi[0:EP, n % 2, 16 * k:16 * k + 16, :].rearrange("p c v -> p (c v)"),
                                     hot_lo[0:EP, n % 2, 16 * k:16 * k + 16, :].rearrange("p c v -> p (c v)"),
                                     start=c == 0 and k == 0, stop=c == 4 and k == W - 1)
                last.then_inc(S["hist_chunk"], 1)

            def pick_counts(n):
                d = n // 2
                if n % 2 == 0:
                    pe.wait_ge(S["hist_masked"], d + 1)
                    te.matmul(bank[2][:, 0:64], hist_s[:, :], sel_hi, start=True, stop=True).then_inc(S["hist_sum"], 1)
                else:
                    pe.wait_ge(S["hist_picked"], d + 1)
                    te.matmul(bank[3][0:64, 0:1], hist_c[:, :], one, start=True, stop=True).then_inc(S["hist_total"], 1)

            def turn_block(n, odd):
                pe.wait_ge(S["xh_ready"], n + 1)
                for c in range(KC):
                    at = (odd * KC + c) * P
                    last = te.transpose(ps_t[:, at:at + P], xh[:, 1, c * P:(c + 1) * P], ident[:, :])
                last.then_inc(S["turned"], 1)

            def project_bank(n, k, odd):
                pe.wait_ge(S["proj_out"], PB * n + k + 1)
                for c in range(KC):
                    last = te.matmul(pj[k % 2][:, :], xts[:, odd, c, :], wrel[:, c, 2 * k:2 * k + 2, :].rearrange("p r o -> p (r o)"),
                                     start=c == 0, stop=c == KC - 1)
                last.then_inc(S["proj_done"], 1)

            def project(n, odd, between=None):
                pe.wait_ge(S["xt_ready"], n + 2)
                for k in range(PB):
                    if k == TURN_AT:
                        turn_block(n + 1, 1 - odd)
                    project_bank(n, k, odd)
                    if between is not None:
                        between(k)

            pe.wait_ge(S["pool_const"], 10)
            turn_block(0, 0)
            pe.wait_ge(S["wf_in"], KC * 16)
            for i in range(6):
                def count_between(k):
                    if i < 5 and k % 4 == 3:
                        count_chunk(2 * i + k // 4)
                    if i == 5 and k % 2 == 1:
                        pick_counts(k // 2)

                project(i, i % 2, count_between)
            with pe.Fori(3, (NB - 1) // 2) as j:
                for a in range(2):
                    project(2 * j + a, a)
            project(NB - 1, (NB - 1) % 2)

            def turn_keys(d, lanes, q, to):
                for c in range(4):
                    at = (4 * q + c) * P
                    last = te.transpose(to[:, c * P:(c + 1) * P], lanes[:, at:at + P], ident[:, :])
                last.then_inc(S["keys_out"], 1)

            pe.wait_ge(S["sorted_ready"], 1)
            for q in range(4):
                turn_keys(0, skeys[:, 0, :], q, bank[q])

            def sum_tile(i, t):
                half, s = t // HALF, t % HALF
                if s == 0:
                    pe.wait_ge(S["onehots_ready"], 2 * i + half + 1)
                pe.wait_ge(S["added"], TILES * i + t + (3 if t < 2 else 1))
                pe.wait_ge(gathered[s], 32 * i + 16 * half + 16)
                te.matmul(ring[t % 4][:, 0:D + 1], onehot[:, half, s, :], grow[:, s, :], start=True, stop=True).then_inc(S["mm_done"], 1)

            pe.wait_ge(S["wb_in"], KC * 16)
            pe.wait_ge(S["loop_in"], KC * 16)
            def forward_pass(i, odd, turn_next):
                n = i + NB
                pe.wait_ge(S["xt_ready"], n + 2)
                pe.wait_ge(S["h_ready"], 2 * i + 1)
                for c in range(KC):
                    last = te.matmul(ps_s[:, 0:D], xts[:, odd, c, :], loop_sb[:, c, :], start=c == 0, stop=c == KC - 1)
                last.then_inc(S["self_done"], 1)
                for t in range(2):
                    sum_tile(i, t)
                for k in range(PB):
                    if k == TURN_AT and turn_next:
                        turn_block(n + 1, 1 - odd)
                    project_bank(n, k, odd)
                    for t in range(2 + 4 * k, 2 + 4 * k + 4):
                        sum_tile(i, t)

            with pe.Fori(0, SPLIT // 2) as j:
                for a in range(2):
                    forward_pass(2 * j + a, (a + NB) % 2, True)
            pe.wait_ge(S["sorted_ready"], 2)
            pe.wait_ge(S["xt_ready"], SPLIT + NB + 2)
            for q in range(4):
                if q:
                    pe.wait_ge(S["keys_copied"], 4 + q)
                turn_keys(1, held[:, 0, :], q, ps_t)
            pe.wait_ge(S["keys_copied"], 8)
            with pe.Fori(SPLIT // 2, (NB - 1) // 2) as j:
                for a in range(2):
                    forward_pass(2 * j + a, (a + NB) % 2, True)
            forward_pass(NB - 1, (2 * NB - 1) % 2, False)
            with pe.Fori(PASSES, 2 * PASSES) as i:
                for t in range(TILES):
                    sum_tile(i, t)
            def norm_chunk(c):
                with pe.Fori(CHUNK * c, CHUNK * (c + 1)) as i:
                    pe.wait_ge(S["xt2_ready"], i + 1)
                    turn_block(i + 2 * NB, 0)
                    pe.wait_ge(S["xt2_ready"], i + 2)
                    for k in range(KC):
                        last = te.matmul(ps_s[:, bass.ds(i, 1)], xts[:, 0, k, :], wr_sb[:, k:k + 1],
                                         start=k == 0, stop=k == KC - 1)
                    last.then_inc(S["wt_done"], 1)

            def count_round(n):
                if n == 0:
                    pe.wait_ge(S["pool_const"], 13)
                pe.wait_ge(S["wt_ready"], n + 1)
                if n < 8:
                    te.matmul(ps_t[:, 0:WAYS], ones[:, :], cnt_f[:, 1, :], start=True, stop=True).then_inc(S["cnt_done"], 1)
                else:
                    te.matmul(ps_t[:, 0:2 * NB], ones[:, :], tie[:, 0:2, :].rearrange("p a b -> p (a b)"), start=True, stop=True)
                    te.matmul(ps_t[:, 2 * NB:3 * NB], tri[:, :], tie[:, 1, :], start=True, stop=True).then_inc(S["cnt_done"], 1)

            def ffn_group(g, blocks, rounds=0):
                for m in range(HC):
                    if m >= 2:
                        pe.wait_ge(S["hid_ready"], g * HC + m - 1)
                    for c in range(KC):
                        last = te.matmul(bank[m % 2][:, 0:blocks * P], w1_sb[:, c, m * P:(m + 1) * P],
                                         xt2[:, bass.ds(g * 4, blocks), c, :], start=c == 0, stop=c == KC - 1)
                    last.then_inc(S["hid_done"], 1)
                    if rounds and m % 2:
                        count_round(m // 2)
                for q in range(blocks):
                    for m in range(HC):
                        if q == 0:
                            pe.wait_ge(S["hid_ready"], g * HC + m + 1)
                        last = te.matmul(bank[2 + q][:, 0:D], hid[:, m, q * P:(q + 1) * P], w2_sb[:, m, :],
                                         start=m == 0, stop=m == HC - 1)
                    last.then_inc(S["y_done"], 1)
                    if rounds:
                        count_round(4 + q)

            norm_chunk(0)
            pe.wait_ge(S["ffn_in"], 32)
            for g in range(EARLY):
                if g:
                    pe.wait_ge(S["y_out"], 4 * g)
                ffn_group(g, 4, rounds=9 if g == EARLY - 1 else 0)
                for c in range(2 * g + 1, min(2 * g + 3, NB // CHUNK)):
                    norm_chunk(c)
            pe.wait_ge(S["y_out"], 4 * EARLY)
            count_round(8)
            ffn_group(EARLY, 4)
            with pe.Fori(EARLY + 1, NB // 4) as g:
                pe.wait_ge(S["fin_ready"], 4 * g + 1)
                ffn_group(g, 4)
            pe.wait_ge(S["fin_ready"], NB)
            ffn_group(NB // 4, 1)


INS = {"x": "x", "src": "src", "dst": "dst", "etype": "edge_type_16", "wf": "L0_gnn_Wf", "wb": "L0_gnn_Wb",
       "loop_w": "L0_gnn_loop_weight", "fwd_bias": "L0_gnn_forward_bias", "bwd_bias": "L0_gnn_backward_bias",
       "self_bias": "L0_gnn_self_bias", "wr": "L0_ffn_wr", "br": "L0_ffn_br", "w1": "L0_ffn_w1",
       "b1": "L0_ffn_b1", "w2": "L0_ffn_w2", "b2": "L0_ffn_b2"}


def kernel(**inputs):
    import concourse.bacc as bacc
    from concourse.bass_utils import run_bass_kernel_spmd

    nc = bacc.Bacc("TRN2", target_bir_lowering=False, num_devices=1)
    arrays, args = {}, {}
    for name, given in INS.items():
        a = np.ascontiguousarray(inputs[given])
        arrays[f"in_{name}"] = a
        args[name] = nc.dram_tensor(f"in_{name}", a.shape, mybir.dt.from_np(a.dtype), kind="ExternalInput").ap()
    n, d = inputs["x"].shape
    rels = inputs["L0_gnn_Wf"].shape[0]
    rows = -(-n // P) * P * rels
    for name in ("table_f", "table_b"):
        args[name] = nc.dram_tensor(name, (rows, d), F32).ap()
    args["x_self"] = nc.dram_tensor("x_self", (-(-n // P) * P, d), F32).ap()
    args["out"] = nc.dram_tensor("out_0", (n, d), F32, kind="ExternalOutput").ap()
    gnn_ffn_kernel(nc, **args)
    r = run_bass_kernel_spmd(nc, [arrays], core_ids=[0])
    return np.asarray(r.results[0]["out_0"])
```

```python
from contextlib import ExitStack

import numpy as np

import concourse.bass as bass
from concourse import mybir

F32 = mybir.dt.float32
BF16 = mybir.dt.bfloat16
I32 = mybir.dt.int32
ALU = mybir.AluOpType
ACT = mybir.ActivationFunctionType
AX = mybir.AxisListType

P = 128

TOP = 0x40000000
ROW_BITS = 17
LANE_BITS = 11
LANE = 1 << LANE_BITS
TILES = 34
HALF = TILES // 2
HIST = 336
EPS = 1e-5


def bits_as_float(v):
    return float(np.array([v], np.uint32).view(np.float32)[0])


def gnn_ffn_kernel(nc, x, src, dst, etype, wf, wb, loop_w, fwd_bias, bwd_bias, self_bias,
                   wr, br, w1, b1, w2, b2, table_f, table_b, x_self, out):
    N, D = x.shape
    E = src.shape[0]
    R = wf.shape[0]
    H = w1.shape[1]
    NB = -(-N // P)
    LAST = N - (NB - 1) * P
    KC = D // P
    HC = H // P
    PAD_ROW = N * R
    EP = 125
    EC = E // EP
    PADS = P - 1
    PASSES = NB
    KEYS = 107 * 16
    K_TOP = max(1, N // 2) - 1
    assert EP * EC == E and EC + PADS <= LANE and N <= 1 << 13 and D == 256
    assert NB % 7 == 0 and NB % 4 == 1
    assert PASSES * TILES * P >= E + NB * PADS and KEYS >= (PASSES + 1) * TILES
    SENTINEL = TOP | (NB << 24) | PAD_ROW
    PB = R * D // 512
    PARTS = 21
    ROW_STAGES = LANE_BITS * (LANE_BITS + 1) // 2 + 1
    ROW_PASSES = 14
    MERGE_PASSES = 4
    SPLIT = ROW_PASSES + 7 * MERGE_PASSES
    RING = 22
    SELF_AT = 6
    TURN_AT = PB - 2
    AHEAD = 14
    CHUNK = 7
    EARLY = 4
    NORMS = 2 * CHUNK
    assert (EARLY - 1) * NORMS + CHUNK == NB
    WAYS = 15
    ROW_SHARE = 10
    MERGE_SHARE = 11
    assert ROW_PASSES * ROW_SHARE >= 2 * ROW_STAGES and MERGE_PASSES * MERGE_SHARE >= 2 * PARTS
    assert 3 * MERGE_SHARE <= TILES and (RING - ROW_PASSES) % MERGE_PASSES == 0

    with ExitStack() as ctx:
        def sb(name, shape, dt=F32):
            return ctx.enter_context(nc.sbuf_tensor(name, shape, dt))

        def pb(name, shape, dt=F32):
            return ctx.enter_context(nc.psum_tensor(name, shape, dt))

        def sem(name):
            return ctx.enter_context(nc.semaphore(name))

        h_mem = sb("h_mem", [P, NB * D])
        h = h_mem[:, :].rearrange("p (b d) -> p b d", d=D)
        acc_mem = sb("acc_mem", [P, NB * (D + 1)])
        acc = acc_mem[:, :].rearrange("p (b c) -> p b c", c=D + 1)
        skeys = acc_mem[:, 0:2 * LANE].rearrange("p (a f) -> p a f", a=2)
        skeys_i = skeys.bitcast(I32)
        HELD_AT = NB - 3 * LANE // D
        held = h_mem[:, HELD_AT * D:NB * D].rearrange("p (a f) -> p a f", a=3)
        assert RING % 2 == 0 and SPLIT % 2 == 0 and RING + 2 <= HELD_AT <= SPLIT + 2
        work = [acc_mem[:, (2 + a) * LANE:(3 + a) * LANE] for a in range(2)]
        work_i = [w.bitcast(I32) for w in work]
        typ_i = acc_mem[:, 4 * LANE:4 * LANE + EC].bitcast(I32)
        xt2 = acc_mem[:, 0:NB * KC * P].rearrange("p (b c n) -> p b c n", b=NB, c=KC)
        w_mem = sb("w_mem", [P, KC * R * D])
        wrel = w_mem[:, :].rearrange("p (c r o) -> p c r o", c=KC, r=R)
        w1_sb = w_mem[:, 0:KC * H].rearrange("p (c m) -> p c m", c=KC)
        w2_sb = w_mem[:, KC * H:KC * H + HC * D].rearrange("p (c o) -> p c o", c=HC)
        g_mem = sb("g_mem", [P, HALF * (D + 1)])
        grow = g_mem[:, :].rearrange("p (s c) -> p s c", c=D + 1)
        hot_hi = g_mem[:, 0:HIST * 8].bitcast(BF16).rearrange("p (a c v) -> p a c v", a=2, v=8)
        oh_mem = sb("oh_mem", [P, 2 * HALF * P])
        onehot = oh_mem[:, :].rearrange("p (a s n) -> p a s n", a=2, s=HALF)
        hot_lo = oh_mem[:, 0:HIST * 8].bitcast(BF16).rearrange("p (a c v) -> p a c v", a=2, v=8)
        hid = oh_mem[:, 0:HC * 512].rearrange("p (c n) -> p c n", c=HC)
        stage = sb("stage", [P, 2, R * D // 2])
        keys = sb("keys", [P, PASSES * TILES + KEYS], I32)
        ends_i = [keys[:, a * EC:(a + 1) * EC] for a in range(2)]
        loop_sb = sb("loop_sb", [P, KC, D])
        ident = sb("ident", [P, P])
        iota_f = sb("iota_f", [P, P])
        xh = sb("xh", [P, 2, D])
        xts = sb("xts", [P, 2, KC, P])
        bias_bc = sb("bias_bc", [P, 4, D])
        first_at = [4 * LANE + EC]

        def first(size):
            first_at[0] += size
            return acc_mem[:, first_at[0] - size:first_at[0]]

        iota_i = first(P).bitcast(I32)
        one = first(1)
        blkmask = first(P)
        sel_hi = first(64)
        sel_lo = first(64)
        hist_s = first(P)
        hist_c = first(64)
        pad_i = first(P).bitcast(I32)
        stats = first(NB * 6).rearrange("p (b c) -> p b c", c=6)
        sgn3 = sb("sgn3", [P, 3, 8])
        small_i = sb("small_i", [P, 16], I32)
        sgn = sb("sgn", [P, 8])
        sgn2 = sb("sgn2", [P, 8])
        padn = sb("padn", [P, 4])
        stats2 = stage[:, 1, 0:CHUNK * 6].rearrange("p (b c) -> p b c", c=6)
        mv = sb("mv", [P, NB, 2])
        mneg = sb("mneg", [P, NB])
        rstd = sb("rstd", [P, NB])
        lt = sb("lt", [P, NB])
        rows_i = sb("rows_i", [P, 2, HALF + 3], I32)
        loc_i = sb("loc_i", [P, 2, HALF + 3], I32)
        loc_f = sb("loc_f", [P, 2, HALF + 3])
        pad_f = sb("pad_f", [P, 2, HALF + 3])
        blk_i = sb("blk_i", [1, 2, HALF + 3], I32)
        late_at = [0]

        def late(*shape):
            size = int(np.prod(shape))
            at = g_mem[:, late_at[0]:late_at[0] + size]
            late_at[0] += size
            return at if len(shape) == 1 else at.rearrange("p (a b) -> p a b", a=shape[0])

        inv = sb("inv", [P, NB])
        has = sb("has", [P, 2, NB])
        wts = late(NB)
        key_i = late(2, NB).bitcast(I32)
        key_f = late(2, NB)
        cmp_f = stage[:, 0, 0:WAYS * NB].rearrange("p (w b) -> p w b", w=WAYS)
        cnt_f = late(2, WAYS)
        steps_f = late(WAYS + 1)
        thr = sb("thr", [P, 4])
        tie = late(4, NB)
        wr_sb = sb("wr_sb", [P, KC])
        b1_sb = sb("b1_sb", [P, HC])
        br_sb = sb("br_sb", [P, 1])
        wsel = late(NB)
        y_kept = w_mem[:, KC * H + HC * D:KC * H + HC * D + EARLY * 4 * D].rearrange("p (b d) -> p b d", d=D)
        ybuf = late(8, D)
        tri = late(P)
        ones = late(P)

        bank = [pb(f"bank{n}", [P, 512]) for n in range(8)]
        ring = bank[0:4]
        pj = bank[4:6]
        ps_t = bank[6]
        ps_s = bank[7]

        names = ("x_first dst_in x_in edges_in bias_in wf_in wb_in loop_in ffn_in const_ready dve_chain stats_ready "
                 "hot_ready hist_chunk hist_masked hist_sum hist_picked hist_total "
                 "keys_out keys_copied sorted_ready held_free stage_done xh_part xh_ready turned xt_ready "
                 "proj_done proj_out half_ready hot_parts onehots_ready mm_done added self_done h_ready "
                 "ring_out ring_in restored wt_done wt_ready cmp_ready cnt_done y_out loop_chain fin_steps folded zeroed hid_done hid_ready "
                 "y_done fin_ready gather_go blocks_go pool_const xt2_ready").split()
        S = {n: sem(n) for n in names}
        stored = [sem("stored_lo"), sem("stored_hi")]
        stage_free = [sem("stage_free_lo"), sem("stage_free_hi")]
        gathered = [sem(f"gathered{n}") for n in range(HALF)]
        out_done = [sem("out_done0"), sem("out_done1")]

        block = ctx.enter_context(nc.Block())

        @block.sync
        def _(sp):
            for a in range(2):
                sp.sem_inc(stage_free[a], 1)
            sp.sem_inc(S["ring_in"], 16)
            sp.dma_start(h[:, 0:AHEAD, :], x[0:AHEAD * P, :].rearrange("(b p) d -> p b d", p=P)).then_inc(S["x_first"], 16)
            sp.dma_start(ends_i[0][0:EP, :], dst.rearrange("(p c) -> p c", c=EC)).then_inc(S["dst_in"], 16)
            for c in range(KC):
                sp.dma_start(wrel[:, c], wf[:, c * P:(c + 1) * P, :].rearrange("r p o -> p r o")).then_inc(S["wf_in"], 16)
            sp.dma_start(ends_i[1][0:EP, :], src.rearrange("(p c) -> p c", c=EC)).then_inc(S["edges_in"], 16)
            sp.dma_start(typ_i[0:EP, :], etype.rearrange("(p c) -> p c", c=EC)).then_inc(S["edges_in"], 16)
            sp.dma_start(h[:, AHEAD:NB - 1, :], x[AHEAD * P:(NB - 1) * P, :].rearrange("(b p) d -> p b d", p=P)).then_inc(S["x_in"], 16)
            sp.wait_ge(S["const_ready"], 1)
            sp.dma_start(h[0:LAST, NB - 1, :], x[(NB - 1) * P:N, :]).then_inc(S["x_in"], 16)
            for c in range(KC):
                sp.dma_start(loop_sb[:, c], loop_w[c * P:(c + 1) * P, :]).then_inc(S["loop_in"], 16)
                sp.dma_start(wr_sb[:, c:c + 1], wr[c * P:(c + 1) * P, :]).then_inc(S["bias_in"], 16)
            for n, b in enumerate((fwd_bias, bwd_bias, self_bias, b2)):
                sp.dma_start(bias_bc[:, n, :], b.rearrange("(a d) -> a d", a=1).broadcast_to([P, D])).then_inc(S["bias_in"], 16)
            sp.dma_start(b1_sb[:, :], b1.rearrange("(c p) -> p c", p=P), allow_slow_non_contiguous=True).then_inc(S["bias_in"], 16)
            sp.dma_start(br_sb[:, :], br.rearrange("(a d) -> a d", a=1).broadcast_to([P, 1])).then_inc(S["bias_in"], 16)

            def turn_ring(i, slot, following):
                at = h[:, RING + slot, :]
                sp.wait_ge(S["h_ready"], 2 * i + 3)
                sp.dma_start(x_self[bass.ds(i * P, P), :], at).then_inc(S["ring_out"], 16)
                if following:
                    sp.wait_ge(S["ring_out"], (i - RING + 1) * 16)
                    sp.dma_start(at, x[bass.ds((i + 2) * P, P), :]).then_inc(S["ring_in"], 16)

            def restore(start, stop):
                sp.dma_start(h[:, start:stop, :], x_self[start * P:stop * P, :].rearrange("(b p) d -> p b d", p=P)).then_inc(S["restored"], 16)

            def store_block(table, i, n, between=None):
                t = table.rearrange("(b p r) d -> b p (r d)", p=P, r=R)
                for a in range(2):
                    sp.wait_ge(S["proj_out"], n * PB + (a + 1) * (PB // 2) + 2)
                    sp.dma_start(t[bass.ds(i, 1), :, a * (R * D // 2):(a + 1) * (R * D // 2)].rearrange("a p f -> (a p) f"),
                                 stage[:, a, :]).then_inc(stored[a], 16)
                    sp.wait_ge(stored[a], (n + 1) * 16)
                    sp.sem_inc(stage_free[a], 1)
                    if a == 0 and between is not None:
                        between()

            with sp.Fori(0, NB) as i:
                store_block(table_f, i, i)
            sp.wait_ge(S["proj_done"], NB * PB)
            for c in range(KC):
                sp.dma_start(wrel[:, c], wb[:, c * P:(c + 1) * P, :].rearrange("r p o -> p r o")).then_inc(S["wb_in"], 16)
            with sp.Fori(0, RING) as i:
                store_block(table_b, i, i + NB)
            with sp.Fori(RING // 2, SPLIT // 2) as j:
                for a in range(2):
                    store_block(table_b, 2 * j + a, 2 * j + a + NB, lambda: turn_ring(2 * j + a, a, True))
            sp.wait_ge(S["held_free"], 1)
            sp.dma_start(h[:, SPLIT + 2:NB - 1, :], x[(SPLIT + 2) * P:(NB - 1) * P, :].rearrange("(b p) d -> p b d", p=P)).then_inc(S["x_in"], 16)
            sp.dma_start(h[0:LAST, NB - 1, :], x[(NB - 1) * P:N, :]).then_inc(S["x_in"], 16)
            restore(RING + 2, SPLIT)
            for a in range(2):
                store_block(table_b, SPLIT + a, SPLIT + a + NB, lambda: turn_ring(SPLIT + a, a, False))
            sp.wait_ge(S["ring_out"], (SPLIT + 2 - RING) * 16)
            restore(RING, RING + 2)
            restore(SPLIT, SPLIT + 2)
            with sp.Fori(SPLIT + 2, NB) as i:
                store_block(table_b, i, i + NB)
            sp.wait_ge(S["proj_done"], 2 * NB * PB)
            sp.dma_start(w1_sb, w1.rearrange("(c p) m -> p c m", p=P)).then_inc(S["ffn_in"], 16)
            sp.dma_start(w2_sb, w2.rearrange("(c p) o -> p c o", p=P)).then_inc(S["ffn_in"], 16)
            with sp.Fori(0, (NB - 1) // 2) as i:
                for a in range(2):
                    sp.wait_ge(S["fin_ready"], 2 * i + a + 2)
                    sp.dma_start(out[bass.ds(i * 2 * P + a * P, P), :], h[:, bass.ds(2 * i + a, 1), :].rearrange("p a d -> p (a d)")).then_inc(out_done[a], 16)
            sp.wait_ge(S["fin_ready"], NB + 1)
            sp.dma_start(out[(NB - 1) * P:N, :], h[0:LAST, NB - 1, :]).then_inc(out_done[0], 16)
            sp.wait_ge(out_done[0], ((NB - 1) // 2 + 1) * 16)
            sp.wait_ge(out_done[1], ((NB - 1) // 2) * 16)

        @block.gpsimd
        def _(pool):
            g = nc.gpsimd
            g.memset(h[:, NB - 1, :], 0.0).then_inc(S["const_ready"], 1)
            g.iota(iota_i[:, :], pattern=[[1, P]], base=0, channel_multiplier=0).then_inc(S["pool_const"], 1)
            g.iota(small_i[:, 0:8], pattern=[[0, 8]], base=0, channel_multiplier=1).then_inc(S["pool_const"], 1)
            g.iota(pad_i[:, :], pattern=[[1, P]], base=PAD_ROW, channel_multiplier=0).then_inc(S["pool_const"], 1)
            g.memset(ident[:, :], 0.0).then_inc(S["pool_const"], 1)
            g.memset(one, 1.0).then_inc(S["pool_const"], 1)
            pool.wait_ge(S["pool_const"], 5)
            g.affine_select(out=ident[:, :], in_=ident[:, :], compare_op=ALU.not_equal, fill=1.0,
                            base=0, pattern=[[-1, P]], channel_multiplier=1).then_inc(S["pool_const"], 1)
            for hot in (hot_hi, hot_lo):
                for a in range(2):
                    g.memset(hot[:, a, HIST - 6:HIST, :], 0.0).then_inc(S["pool_const"], 1)
            pool.wait_ge(S["hist_chunk"], 2 * (EC // (HIST - 6)))
            g.memset(grow[:, :, D:D + 1], 1.0).then_inc(S["pool_const"], 1)

            def gather(table, i):
                for t in range(TILES):
                    half, s = t // HALF, t % HALF
                    pool.wait_ge(S["mm_done"], TILES * i + t + 1)
                    if s == 0:
                        pool.wait_ge(S["half_ready"], 2 * i + half + 1)
                    pool.sem_inc(S["gather_go"], 1)
                    g.indirect_dma_start(grow[:, s, 0:D], None, table,
                                         bass.IndirectOffsetOnAxis(rows_i[:, half, s:s + 1], 0)).then_inc(gathered[s], 16)

            pool.wait_ge(S["pool_const"], 11)
            for a in range(2):
                pool.wait_ge(stored[a], NB * 16)
            with pool.Fori(0, PASSES) as i:
                gather(table_f, i)
            for a in range(2):
                pool.wait_ge(stored[a], 2 * NB * 16)
            with pool.Fori(PASSES, 2 * PASSES) as i:
                gather(table_b, i)
            pool.wait_ge(S["mm_done"], 2 * PASSES * TILES + HALF)
            g.memset(ones[:, :], 1.0).then_inc(S["pool_const"], 1)
            pool.wait_ge(S["pool_const"], 12)
            g.affine_select(out=tri[:, :], in_=ones[:, :], compare_op=ALU.is_gt, fill=0.0,
                            base=0, pattern=[[1, P]], channel_multiplier=-1).then_inc(S["pool_const"], 1)

        @block.scalar
        def _(act):
            a_ = nc.scalar
            act.sem_inc(S["proj_out"], 2)
            act.sem_inc(S["xt_ready"], 1)
            act.sem_inc(S["xt2_ready"], 1)
            act.sem_inc(S["y_out"], 4)
            act.wait_ge(S["stats_ready"], 1)

            def norm_block(i, n, at=None):
                act.wait_ge(S["turned"], n + 1)
                a_.activation(xh[:, 0, :], h[:, bass.ds(i if at is None else at, 1), :].rearrange("p a d -> p (a d)"), ACT.Identity,
                              bias=mneg[:, bass.ds(i, 1)]).then_inc(S["xh_part"], 1)
                act.wait_ge(S["xh_part"], n + 1)
                a_.activation(xh[:, 1, :], xh[:, 0, :], ACT.Copy, scale=rstd[:, bass.ds(i, 1)]).then_inc(S["xh_ready"], 1)

            def copy_turned(n, odd):
                act.wait_ge(S["turned"], n + 2)
                a_.activation(xts[:, odd, :, :].rearrange("p c n -> p (c n)"), ps_t[:, odd * KC * P:(odd + 1) * KC * P],
                              ACT.Copy).then_inc(S["xt_ready"], 1)

            def one_hots(i, half):
                act.wait_ge(S["half_ready"], 2 * i + half + 1)
                for s in range(HALF):
                    a_.activation(onehot[:, half, s, :], iota_f[:, :], ACT.Abs, bias=loc_f[:, half, s:s + 1]).then_inc(S["hot_parts"], 1)
                act.wait_ge(S["hot_parts"], (2 * i + half + 1) * HALF)
                both = onehot[:, half, :, :].rearrange("p s n -> p (s n)")
                a_.activation(both, both, ACT.Relu, scale=-1.0, bias=1.0).then_inc(S["onehots_ready"], 1)

            def project_out(n, following, odd, i=None, slot=None):
                if following is not None:
                    norm_block(following, n + 1, slot)
                for k in range(PB):
                    half, at = k // (PB // 2), k % (PB // 2) * 512
                    if k == TURN_AT and following is not None:
                        copy_turned(n + 1, 1 - odd)
                    act.wait_ge(S["proj_done"], n * PB + k + 1)
                    if at == 0:
                        act.wait_ge(stage_free[half], n + 1)
                    a_.activation(stage[:, half, at:at + 512], pj[k % 2][:, :], ACT.Copy).then_inc(S["proj_out"], 1)
                    if i is not None and k == 4:
                        one_hots(i + 1, 0)
                if i is not None:
                    one_hots(i + 1, 1)

            def project_pairs(start, stop, base):
                with act.Fori(start // 2, stop // 2) as j:
                    for a in range(2):
                        project_out(2 * j + a + base, 2 * j + a + 1, (a + base) % 2, 2 * j + a if base else None)

            norm_block(0, 0)
            copy_turned(0, 0)
            project_pairs(0, AHEAD - 2, 0)
            act.wait_ge(S["stats_ready"], 2)
            project_pairs(AHEAD - 2, NB - 1, 0)
            project_out(NB - 1, 0, (NB - 1) % 2)
            for half in range(2):
                one_hots(0, half)
            project_pairs(0, RING, NB)

            def project_ring(i, a):
                act.wait_ge(S["ring_in"], (i + 1 - RING) * 16)
                project_out(i + NB, i + 1, (a + NB) % 2, i, RING + 1 - a)

            with act.Fori(RING // 2, SPLIT // 2) as j:
                for a in range(2):
                    project_ring(2 * j + a, a)
            project_ring(SPLIT, 0)
            act.wait_ge(S["x_in"], 64)
            project_out(SPLIT + 1 + NB, SPLIT + 2, (1 + NB) % 2, SPLIT + 1)
            project_pairs(SPLIT + 2, NB - 1, NB)
            project_out(2 * NB - 1, None, (2 * NB - 1) % 2, NB - 1)
            with act.Fori(0, NB // CHUNK) as c:
                act.wait_ge(S["folded"], c + 1)
                a_.activation(acc[:, bass.ds(c * CHUNK, CHUNK), :].rearrange("p b c -> p (b c)"),
                              iota_f[:, 0:1].broadcast_to([P, CHUNK * (D + 1)]), ACT.Copy).then_inc(S["zeroed"], 1)
            with act.Fori(PASSES, 2 * PASSES - 1) as i:
                for half in range(2):
                    one_hots(i + 1, half)

            def copy_late(i, odd):
                copy_turned(i + 2 * NB, odd)
                a_.activation(xt2[:, bass.ds(i, 1)].rearrange("p a c n -> p (a c n)"), ps_t[:, odd * KC * P:(odd + 1) * KC * P],
                              ACT.Copy).then_inc(S["xt2_ready"], 1)

            def hidden(g, width, between=None):
                for m in range(HC):
                    act.wait_ge(S["hid_done"], g * HC + m + 1)
                    a_.activation(hid[:, m, 0:width], bank[m % 2][:, 0:width], ACT.Gelu_apprx_tanh,
                                  bias=b1_sb[:, m:m + 1]).then_inc(S["hid_ready"], 1)
                    if between is not None:
                        between(m)

            def keep(g, between=None):
                for q in range(4):
                    if between is not None:
                        between(2 * q)
                    act.wait_ge(S["y_done"], 4 * g + q + 1)
                    a_.activation(y_kept[:, bass.ds(4 * g + q, 1), :].rearrange("p a d -> p (a d)"), bank[2 + q][:, 0:D],
                                  ACT.Copy).then_inc(S["y_out"], 1)
                    if between is not None:
                        between(2 * q + 1)

            act.wait_ge(S["stats_ready"], 3)
            norm_block(0, 2 * NB)
            for i in range(CHUNK):
                if i + 1 < CHUNK:
                    norm_block(i + 1, i + 1 + 2 * NB)
                copy_late(i, i % 2)
            act.wait_ge(S["ffn_in"], 32)
            with act.Fori(0, EARLY - 1) as g:
                def norm_next(n):
                    i = CHUNK + NORMS * g + n
                    if 0 < n <= NORMS:
                        copy_late(i - 1, (CHUNK + n - 1) % 2)
                    if n < NORMS:
                        if n % CHUNK == 0:
                            act.wait_ge(S["stats_ready"], 2 * g + n // CHUNK + 4)
                        norm_block(i, i + 2 * NB)

                hidden(g, 4 * P, norm_next)
                keep(g, lambda k: norm_next(HC + k))
            hidden(EARLY - 1, 4 * P)
            keep(EARLY - 1)
            with act.Fori(EARLY, NB // 4) as g:
                act.wait_ge(S["y_done"], 4 * g)
                hidden(g, 4 * P)
            act.wait_ge(S["y_done"], NB - 1)
            hidden(NB // 4, P)

        @block.vector
        def _(dve):
            v = nc.vector
            links = [0]
            for name in ("h_ready", "fin_ready"):
                dve.sem_inc(S[name], 1)

            def link(*ins):
                for x_ in ins:
                    links[0] += 1
                    x_.then_inc(S["dve_chain"], 1)
                dve.wait_ge(S["dve_chain"], links[0])

            dve.wait_ge(S["pool_const"], 10)
            link(v.memset(skeys[:, :, :], bits_as_float(SENTINEL)),
                 v.tensor_copy(iota_f[:, :], iota_i[:, :]))

            def statistics(b):
                return v.bn_stats(stats[:, b, :], h[:, b, :])

            local = [0]

            def step(*ins):
                for x_ in ins:
                    local[0] += 1
                    x_.then_inc(S["loop_chain"], 1)
                dve.wait_ge(S["loop_chain"], local[0])

            def end_steps():
                local[0] = 0
                dve.sem_clear(S["loop_chain"])

            def finish_statistics(mean, var, neg, inv_std, t):
                step(v.tensor_scalar(neg, mean, -1.0, None, ALU.mult),
                     v.tensor_scalar(var, var, 1.0, EPS, ALU.mult, ALU.add))
                step(v.tensor_scalar(t.bitcast(I32), var.bitcast(I32), 1, None, ALU.logical_shift_right))
                step(v.tensor_scalar(inv_std.bitcast(I32), t.bitcast(I32), -1.0, float(0x5F3759DF), ALU.mult, ALU.add))
                for _ in range(3):
                    step(v.tensor_tensor(t, inv_std, inv_std, ALU.mult))
                    step(v.tensor_tensor(t, t, var, ALU.mult))
                    step(v.tensor_scalar(t, t, -0.5, 1.5, ALU.mult, ALU.add))
                    step(v.tensor_tensor(inv_std, inv_std, t, ALU.mult))

            def first_statistics(start, stop):
                link(*[statistics(b) for b in range(start, stop)])
                link(*[v.bn_aggr(mv[:, b, :], stats[:, b, :]) for b in range(start, stop)])
                link(v.tensor_copy(inv[:, start:stop], mv[:, start:stop, 1]))
                finish_statistics(mv[:, start:stop, 0], inv[:, start:stop], mneg[:, start:stop], rstd[:, start:stop],
                                  lt[:, start:stop])
                end_steps()
                v.tensor_copy(padn[:, 3:4], iota_f[:, 0:1]).then_inc(S["stats_ready"], 1)

            dve.wait_ge(S["x_first"], 16)
            first_statistics(0, AHEAD)

            link(*[v.tensor_scalar(small_i[:, 8 + b:9 + b], small_i[:, b:b + 1], b, 1,
                                   ALU.logical_shift_right, ALU.bitwise_and) for b in range(7)])
            link(v.tensor_scalar(sgn[:, 0:7], small_i[:, 8:15], -2.0, 1.0, ALU.mult, ALU.add))
            link(v.tensor_tensor(sgn2[:, 1:7], sgn[:, 0:6], sgn[:, 1:7], ALU.mult))
            link(v.tensor_scalar(hist_s[:, :].bitcast(I32), iota_i[:, :], 3, None, ALU.logical_shift_right),
                 v.tensor_scalar(small_i[:, 8:9], small_i[:, 0:1], 3, None, ALU.logical_shift_right),
                 v.tensor_scalar(small_i[:, 9:10], small_i[:, 0:1], 7, None, ALU.bitwise_and),
                 v.tensor_scalar(hist_c[:, :].bitcast(I32), iota_i[:, 0:64], 7, None, ALU.bitwise_and))
            link(v.tensor_copy(padn[:, 0:2], small_i[:, 8:10]),
                 v.tensor_copy(iota_f[:, :], hist_s[:, :].bitcast(I32)),
                 v.tensor_copy(sel_lo, hist_c[:, :].bitcast(I32)))
            link(v.tensor_scalar(blkmask, iota_f[:, :], padn[:, 0:1], None, ALU.is_equal),
                 v.tensor_scalar(sel_hi, iota_f[:, 0:64], padn[:, 1:2], None, ALU.is_equal),
                 v.tensor_scalar(sel_lo, sel_lo, padn[:, 1:2], None, ALU.is_equal))
            link(v.tensor_copy(iota_f[:, :], iota_i[:, :]))

            W = HIST - 6
            for d in range(2):
                if d == 0:
                    dve.wait_ge(S["dst_in"], 16)
                else:
                    dve.wait_ge(S["edges_in"], 32)
                node = ends_i[d][0:EP, :]
                link(v.tensor_scalar(work_i[0][0:EP, 0:EC], node, 10, None, ALU.logical_shift_right),
                     v.tensor_scalar(work_i[1][0:EP, 0:EC], node, 7, 7, ALU.logical_shift_right, ALU.bitwise_and))
                for c in range(EC // W):
                    n = d * (EC // W) + c
                    if n >= 2:
                        dve.wait_ge(S["hist_chunk"], n - 1)
                    for digit, hot in ((0, hot_hi), (1, hot_lo)):
                        v.tensor_tensor(hot[0:EP, n % 2, 0:W, :],
                                        work_i[digit][0:EP, c * W:(c + 1) * W].unsqueeze(2).broadcast_to([EP, W, 8]),
                                        iota_f[0:EP, 0:8].unsqueeze(1).broadcast_to([EP, W, 8]),
                                        ALU.is_equal).then_inc(S["hot_ready"], 1)
                dve.wait_ge(S["hot_ready"], 2 * (d + 1) * (EC // W))
                if d == 0:
                    dve.wait_ge(S["x_in"], 32)
                    first_statistics(AHEAD, NB)
            for d in range(2):
                dve.wait_ge(S["hist_chunk"], 2 * (EC // W))
                v.tensor_tensor(hist_s[:, :], bank[d][:, 0:P], blkmask, ALU.mult).then_inc(S["hist_masked"], 1)
                dve.wait_ge(S["hist_sum"], d + 1)
                v.tensor_tensor(hist_c[:, :], bank[2][:, 0:64], sel_lo, ALU.mult).then_inc(S["hist_picked"], 1)
                dve.wait_ge(S["hist_total"], d + 1)
                link(v.tensor_scalar(small_i[0:64, 8:9], bank[3][0:64, 0:1], -1.0, None, ALU.mult))
                link(v.tensor_scalar(small_i[0:64, 9:10], small_i[0:64, 8:9], P - 1, None, ALU.bitwise_and))
                link(v.tensor_copy(padn[0:64, 0:1], small_i[0:64, 9:10]))
                link(v.tensor_scalar(small_i[0:64, 10:11], small_i[0:64, 0:1], 24, TOP, ALU.logical_shift_left, ALU.bitwise_or))
                link(v.tensor_tensor(hist_s[0:64, :].bitcast(I32), pad_i[0:64, :],
                                     small_i[0:64, 10:11].broadcast_to([64, P]), ALU.bitwise_or),
                     v.tensor_scalar(work[0][0:64, 0:P], iota_f[0:64, :], padn[0:64, 0:1], None, ALU.is_lt))
                link(v.copy_predicated(skeys[0:NB, d, EC:EC + PADS], work_i[0][0:NB, 0:PADS],
                                       hist_s[0:NB, 0:PADS]))
                link(v.tensor_scalar(work_i[0][0:EP, 0:EC], ends_i[d][0:EP, :], ROW_BITS, TOP,
                                     ALU.logical_shift_left, ALU.bitwise_or),
                     v.tensor_scalar(work_i[1][0:EP, 0:EC], ends_i[1 - d][0:EP, :], 4, None, ALU.logical_shift_left))
                link(v.tensor_tensor(work_i[0][0:EP, 0:EC], work_i[0][0:EP, 0:EC], work_i[1][0:EP, 0:EC], ALU.bitwise_or))
                link(v.tensor_tensor(skeys_i[0:EP, d, 0:EC], work_i[0][0:EP, 0:EC], typ_i[0:EP, :], ALU.bitwise_or))

            link(v.memset(sgn3[:, :, :], 1.0))
            link(v.tensor_copy(sgn3[:, 0, 0:5], sgn2[:, 1:6]),
                 v.tensor_copy(sgn3[:, 0, 5:6], sgn[:, 6:7]),
                 v.tensor_copy(sgn3[:, 1, 6:7], sgn2[:, 6:7]),
                 v.tensor_copy(sgn3[:, 2, 5:6], sgn[:, 5:6]),
                 v.tensor_copy(sgn3[:, 2, 6:7], sgn[:, 5:6]))
            done = S["stage_done"]
            cur, count, bufs, flips = None, 0, work, 0

            def other():
                nonlocal flips
                flips += 1
                return bufs[flips % 2]

            def put(ins):
                nonlocal count
                count += 1
                ins.then_inc(done, 1)

            def ready():
                if count:
                    dve.wait_ge(done, count)

            def directed_half(m, k, r, to):
                a, b = (y.rearrange("p (g r h t l) -> p g r h t l", r=2, h=1 << (m - 1 - k), t=2, l=1 << k)
                        for y in (cur, to))
                put(v.tensor_tensor(b[:, :, r, :, r, :], a[:, :, r, :, 0, :], a[:, :, r, :, 1, :], ALU.min))
                put(v.tensor_tensor(b[:, :, r, :, 1 - r, :], a[:, :, r, :, 0, :], a[:, :, r, :, 1, :], ALU.max))

            def ascend_half(k, which, to):
                a, b = (y.rearrange("p (h t l) -> p h t l", t=2, l=1 << k) for y in (cur, to))
                put(v.tensor_tensor(b[:, :, which, :], a[:, :, 0, :], a[:, :, 1, :], (ALU.min, ALU.max)[which]))

            def ascend(k, to=None):
                nonlocal cur
                ready()
                to = other() if to is None else to
                for which in range(2):
                    ascend_half(k, which, to)
                cur = to

            def negate(sign):
                nonlocal cur
                ready()
                to = other()
                put(v.tensor_scalar(to, cur, sign, None, ALU.mult))
                cur = to

            def turn():
                nonlocal cur
                ready()
                to = other()
                put(v.transpose(to, cur))
                cur = to

            def quadrants(bit):
                nonlocal cur
                ready()
                to = other()
                for q in range(4):
                    w = q ^ bit
                    put(v.tensor_scalar(to[32 * q:32 * q + 32], cur[32 * w:32 * w + 32], -1.0, None, ALU.mult))
                ready()
                put(v.tensor_tensor(to, cur, to, ALU.min))
                cur = to

            row_stages = [(m, k) for m in range(1, LANE_BITS) for k in reversed(range(m))] + [None]
            row_stages += [(LANE_BITS, k) for k in reversed(range(LANE_BITS))]
            assert len(row_stages) == ROW_STAGES

            def row_half(n, lanes):
                nonlocal cur, count
                stage_n, half = n // 2, n % 2
                if n == 0:
                    cur, count = lanes, 0
                if row_stages[stage_n] is None:
                    if half == 0:
                        negate(sgn[:, 0:1])
                    return
                m, k = row_stages[stage_n]
                final = stage_n == ROW_STAGES - 1
                if half == 0:
                    ready()
                    other()
                to = lanes if final else bufs[flips % 2]
                if m < LANE_BITS:
                    directed_half(m, k, half, to)
                else:
                    ascend_half(k, half, to)
                if half == 1:
                    cur = to
                    if final:
                        ready()
                        dve.sem_clear(done)

            def only_from(c, least, step):
                nonlocal cur, count, flips
                ready()
                was = cur, count, flips
                with dve.If(c >= least):
                    step()
                now = cur, count, flips
                with dve.Else():
                    if now[2] % 2 != was[2] % 2:
                        v.tensor_copy(now[0], was[0]).then_inc(done, now[1] - was[1])
                    else:
                        dve.sem_inc(done, now[1] - was[1])

            def merge_half(c, part, half, lanes):
                nonlocal cur, count
                plain = part in range(8, 15) or part > 15
                if plain:
                    k = 0 if part == 8 else LANE_BITS + 8 - part if part < 15 else 20 - part
                    if half == 0:
                        ready()
                        ascend_half(k, 0, lanes if part == 20 else other())
                    else:
                        to = lanes if part == 20 else bufs[flips % 2]
                        ascend_half(k, 1, to)
                        cur = to
                    if part == 20 and half == 1:
                        ready()
                        dve.sem_clear(done)
                elif half == 1:
                    return
                elif part == 0:
                    cur, count = lanes, 0
                    negate(sgn3[:, 0, bass.ds(c, 1)])
                elif part == 1:
                    only_from(c, 6, lambda: (quadrants(2), negate(sgn3[:, 1, bass.ds(c, 1)])))
                elif part == 2:
                    only_from(c, 5, lambda: (quadrants(1), negate(sgn3[:, 2, bass.ds(c, 1)])))
                elif part in (3, 15):
                    turn()
                else:
                    only_from(c, 8 - part, lambda: ascend(8 - part))

            for n in range(2 * ROW_STAGES):
                row_half(n, skeys[:, 0, :])
            with dve.Fori(0, 7) as c:
                for part in range(PARTS):
                    for half in range(2):
                        merge_half(c, part, half, skeys[:, 0, :])
            v.tensor_copy(small_i[:, 8:9], small_i[:, 0:1]).then_inc(S["sorted_ready"], 1)
            def copy_keys(d, q, source):
                dve.wait_ge(S["keys_out"], 4 * d + q + 1)
                to = keys[:, d * PASSES * TILES:d * PASSES * TILES + KEYS].rearrange("p (r c) -> p c r", c=16)
                v.tensor_copy(to[:, 4 * q:4 * q + 4, :],
                              source[:, :].bitcast(I32).rearrange("p (c r) -> p c r", c=4)[:, :, 0:KEYS // 16]).then_inc(S["keys_copied"], 1)

            for q in range(4):
                copy_keys(0, q, bank[q])
            dve.wait_ge(S["keys_copied"], 4)

            def stage_half(i, half, wait):
                kt = keys[:, bass.ds(i * TILES + half * HALF, HALF)]
                v.tensor_scalar(rows_i[:, half, 0:HALF], kt, (1 << ROW_BITS) - 1, None, ALU.bitwise_and).then_inc(S["cmp_ready"], 1)
                v.tensor_scalar(loc_i[:, half, 0:HALF], kt, ROW_BITS, P - 1, ALU.logical_shift_right, ALU.bitwise_and).then_inc(S["cmp_ready"], 1)
                v.tensor_scalar(blk_i[0:1, half, 0:HALF], kt[0:1, :], 24, 63,
                                ALU.logical_shift_right, ALU.bitwise_and).then_inc(S["cmp_ready"], 1)
                dve.wait_ge(S["cmp_ready"], wait + 3)
                v.tensor_scalar(pad_f[:, half, 0:HALF], rows_i[:, half, 0:HALF], float(PAD_ROW), -1000.0,
                                ALU.is_ge, ALU.mult).then_inc(S["cmp_ready"], 1)
                v.tensor_scalar(blk_i[0:1, half, 0:HALF], blk_i[0:1, half, 0:HALF], float(NB - 1), None, ALU.min).then_inc(S["cmp_ready"], 1)
                dve.wait_ge(S["cmp_ready"], wait + 5)
                v.tensor_tensor(loc_f[:, half, 0:HALF], pad_f[:, half, 0:HALF], loc_i[:, half, 0:HALF], ALU.subtract).then_inc(S["half_ready"], 1)

            for half in range(2):
                stage_half(0, half, 5 * half)
            dve.wait_ge(S["turned"], NB + 2)
            link(v.tensor_copy(held[:, 0, :], skeys[:, 1, :]))
            link(v.memset(acc_mem[:, :], 0.0))
            dve.sem_inc(S["added"], 4)

            def load_blocks(i, half):
                dve.wait_ge(S["half_ready"], 2 * i + half + 1)
                dve.sem_inc(S["blocks_go"], 1)
                _, blocks = nc.values_load_multi_w_load_instructions(
                    blk_i[0:1, half, 0:HALF], engines=(mybir.EngineType.DVE,), min_val=0, max_val=NB - 1,
                    skip_runtime_bounds_check_because="the block is masked to six bits and clamped to the last one")
                return blocks

            def add_tile(i, t, blk):
                dve.wait_ge(S["mm_done"], TILES * i + t + HALF + 1)
                dve.wait_ge(S["added"], TILES * i + t + 4)
                to = acc[:, bass.ds(blk, 1), :].rearrange("p a c -> p (a c)")
                v.tensor_tensor(to, ring[t % 4][:, 0:D + 1], to, ALU.add).then_inc(S["added"], 1)

            def self_loop(i, at):
                hb = h[:, bass.ds(at, 1), :].rearrange("p a d -> p (a d)")
                dve.wait_ge(S["self_done"], i + 1)
                v.scalar_tensor_tensor(out=hb, in0=ps_s[:, 0:D], scalar=2.0, in1=hb, op0=ALU.mult, op1=ALU.add).then_inc(S["h_ready"], 1)
                dve.wait_ge(S["h_ready"], 2 * i + 2)
                v.tensor_tensor(hb, hb, bias_bc[:, 2, :], ALU.add).then_inc(S["h_ready"], 1)

            def add_tiles(i, between=None, at=None):
                for half in range(2):
                    blocks = load_blocks(i, half)
                    for s in range(HALF):
                        t = half * HALF + s
                        add_tile(i, t, blocks[s])
                        if between is not None:
                            between(t)
                        if t == SELF_AT and at is not None:
                            self_loop(i, at)
                    stage_half(i + 1, half, 10 * (i + 1) + 5 * half)

            dve.wait_ge(S["bias_in"], (KC + 6) * 16)
            bufs = [held[:, 1, :], held[:, 2, :]]
            for i in range(ROW_PASSES):
                def sort_rows(t):
                    n = i * ROW_SHARE + t // 3
                    if t % 3 == 1 and t < 3 * ROW_SHARE and n < 2 * ROW_STAGES:
                        row_half(n, held[:, 0, :])

                add_tiles(i, sort_rows, i)

            def merge_passes(start, stop, ringed):
                with dve.Fori(start, stop) as c:
                    for a in range(MERGE_PASSES):
                        def merge(t):
                            n = MERGE_SHARE * a + t // 3
                            if t % 3 == 1 and n < 2 * PARTS:
                                merge_half(c, n // 2, n % 2, held[:, 0, :])

                        i = ROW_PASSES + MERGE_PASSES * c + a
                        add_tiles(i, merge, RING + a % 2 if ringed else i)

            merge_passes(0, (RING - ROW_PASSES) // MERGE_PASSES, False)
            merge_passes((RING - ROW_PASSES) // MERGE_PASSES, 7, True)
            v.tensor_copy(small_i[:, 8:9], small_i[:, 0:1]).then_inc(S["sorted_ready"], 1)
            for q in range(4):
                copy_keys(1, q, ps_t)
            dve.wait_ge(S["keys_copied"], 8)
            v.memset(h[:, NB - 1, :], 0.0).then_inc(S["held_free"], 1)
            for a in range(2):
                add_tiles(SPLIT + a, None, RING + a)
            with dve.Fori(SPLIT + 2, PASSES) as i:
                add_tiles(i, None, i)

            def fold_scales(d):
                dve.wait_ge(S["added"], (d + 1) * PASSES * TILES + 4)
                dve.wait_ge(S["h_ready"], 2 * NB + 1)
                link(v.tensor_scalar(inv[:, :], acc[:, :, D], 1.0, None, ALU.max),
                     v.tensor_scalar(has[:, d, :], acc[:, :, D], 1.0, None, ALU.min))
                link(v.reciprocal(inv[:, :], inv[:, :]))
                link(v.tensor_tensor(inv[:, :], inv[:, :], has[:, d, :], ALU.mult))

            def fold_sums(c):
                rows = [h[:, bass.ds(c * CHUNK + b, 1), :].rearrange("p a d -> p (a d)") for b in range(CHUNK)]
                step(*[v.scalar_tensor_tensor(
                    out=rows[b], in0=acc[:, bass.ds(c * CHUNK + b, 1), 0:D].rearrange("p a d -> p (a d)"),
                    scalar=inv[:, bass.ds(c * CHUNK + b, 1)], in1=rows[b], op0=ALU.mult, op1=ALU.add) for b in range(CHUNK)])
                return rows

            def fold_bias(d, i):
                hb = h[:, bass.ds(i, 1), :].rearrange("p a d -> p (a d)")
                return v.scalar_tensor_tensor(out=hb, in0=bias_bc[:, d, :], scalar=has[:, d, bass.ds(i, 1)], in1=hb,
                                              op0=ALU.mult, op1=ALU.add)

            dve.wait_ge(S["restored"], 3 * 16)
            fold_scales(0)
            with dve.Fori(0, NB // CHUNK) as c:
                fold_sums(c)
                end_steps()
                v.tensor_copy(padn[:, 3:4], iota_f[:, 0:1]).then_inc(S["folded"], 1)
            dve.wait_ge(S["zeroed"], NB // CHUNK)
            with dve.Fori(PASSES, 2 * PASSES) as i:
                def bias_on_the_way(t):
                    if t == SELF_AT:
                        fold_bias(0, i - PASSES).then_inc(S["h_ready"], 1)

                add_tiles(i, bias_on_the_way)

            dve.wait_ge(S["h_ready"], 3 * NB + 1)
            fold_scales(1)
            with dve.Fori(0, NB // CHUNK) as c:
                rows = fold_sums(c)
                step(*[fold_bias(1, c * CHUNK + b) for b in range(CHUNK)])
                step(*[v.bn_stats(stats2[:, b, :], rows[b]) for b in range(CHUNK)])
                step(*[v.bn_aggr(mv[:, b, :], stats2[:, b, :]) for b in range(CHUNK)])
                step(v.tensor_copy(lt[:, 0:CHUNK], mv[:, 0:CHUNK, 1]))
                finish_statistics(mv[:, 0:CHUNK, 0], lt[:, 0:CHUNK], mneg[:, bass.ds(c * CHUNK, CHUNK)],
                                  rstd[:, bass.ds(c * CHUNK, CHUNK)], lt[:, CHUNK:2 * CHUNK])
                end_steps()
                v.tensor_copy(padn[:, 3:4], iota_f[:, 0:1]).then_inc(S["stats_ready"], 1)

            dve.wait_ge(S["wt_done"], NB)
            link(v.tensor_scalar(wts[:, :], ps_s[:, 0:NB], br_sb[:, 0:1], None, ALU.add))
            link(v.tensor_scalar(wts[:, :], wts[:, :], 0.0, None, ALU.add))
            wt_i = wts[:, :].bitcast(I32)
            link(v.tensor_scalar(key_i[:, 0, :], wt_i, 31, None, ALU.arith_shift_right))
            link(v.tensor_scalar(key_i[:, 0, :], key_i[:, 0, :], -(1 << 31), None, ALU.bitwise_or))
            link(v.tensor_tensor(key_i[:, 0, :], key_i[:, 0, :], wt_i, ALU.bitwise_xor))
            link(v.tensor_scalar(key_i[:, 1, :], key_i[:, 0, :], 0xFFFF, None, ALU.bitwise_and))
            link(v.tensor_scalar(key_i[:, 0, :], key_i[:, 0, :], 16, 0xFFFF, ALU.logical_shift_right, ALU.bitwise_and))
            link(v.tensor_copy(key_f[:, :, :], key_i[:, :, :]))
            link(v.tensor_scalar(key_f[:, 0, NB - 1:NB], key_f[:, 0, NB - 1:NB], 1.0, None, ALU.add))
            link(v.tensor_scalar(thr[:, 2:3], small_i[:, 0:1], float(LAST), None, ALU.is_lt))
            link(v.tensor_scalar(key_f[:, 0, NB - 1:NB], key_f[:, 0, NB - 1:NB], thr[:, 2:3], -1.0, ALU.mult, ALU.add))
            link(v.tensor_scalar(steps_f[:, 0:WAYS], iota_f[:, 1:WAYS + 1], 1.0, None, ALU.mult))
            rounds = 0
            for phase in range(2):
                if phase == 1:
                    link(v.tensor_scalar(tie[:, 0, :], key_f[:, 0, :], thr[:, 0:1], None, ALU.is_equal),
                         v.tensor_scalar(tie[:, 1, :], key_f[:, 0, :], thr[:, 0:1], 65537.0, ALU.is_gt, ALU.mult),
                         v.tensor_scalar(tie[:, 2, :], key_f[:, 1, :], 1.0, None, ALU.add))
                    link(v.tensor_tensor(tie[:, 0, :], tie[:, 0, :], tie[:, 2, :], ALU.mult))
                    link(v.tensor_tensor(tie[:, 0, :], tie[:, 0, :], tie[:, 1, :], ALU.add))
                    link(v.tensor_scalar(key_f[:, 0, :], tie[:, 0, :], -1.0, None, ALU.add))
                link(v.memset(thr[:, 0:1], 0.0))
                for step in (4096.0, 256.0, 16.0, 1.0):
                    link(v.tensor_scalar(cnt_f[:, 0, :], steps_f[:, 0:WAYS], step, thr[:, 0:1], ALU.mult, ALU.add))
                    link(v.tensor_tensor(cmp_f, key_f[:, 0, :].unsqueeze(1).broadcast_to([P, WAYS, NB]),
                                         cnt_f[:, 0, :].unsqueeze(2).broadcast_to([P, WAYS, NB]), ALU.is_ge))
                    v.tensor_reduce(cnt_f[:, 1, :], cmp_f, AX.X, ALU.add).then_inc(S["wt_ready"], 1)
                    rounds += 1
                    dve.wait_ge(S["cnt_done"], rounds)
                    link(v.tensor_scalar(cnt_f[:, 1, :], ps_t[:, 0:WAYS], float(K_TOP), step, ALU.is_ge, ALU.mult))
                    link(v.tensor_reduce(thr[:, 1:2], cnt_f[:, 1, :], AX.X, ALU.add))
                    link(v.tensor_tensor(thr[:, 0:1], thr[:, 0:1], thr[:, 1:2], ALU.add))
            link(v.tensor_scalar(tie[:, 0, :], key_f[:, 0, :], thr[:, 0:1], None, ALU.is_gt))
            v.tensor_scalar(tie[:, 1, :], key_f[:, 0, :], thr[:, 0:1], None, ALU.is_equal).then_inc(S["wt_ready"], 1)
            rounds += 1
            dve.wait_ge(S["cnt_done"], rounds)
            link(v.tensor_reduce(thr[:, 1:2], ps_t[:, 0:NB], AX.X, ALU.add),
                 v.tensor_copy(tie[:, 2, :], ps_t[:, NB:2 * NB]),
                 v.memset(key_f[:, 1, :], 0.0))
            link(v.tensor_scalar(thr[:, 1:2], thr[:, 1:2], -1.0, float(K_TOP), ALU.mult, ALU.add),
                 v.tensor_tensor_scan(tie[:, 3, :], tie[:, 2, :], key_f[:, 1, :], 0.0, ALU.add, ALU.add))
            link(v.tensor_tensor(tie[:, 3, :], tie[:, 3, :], tie[:, 2, :], ALU.subtract))
            link(v.tensor_tensor(tie[:, 3, :], tie[:, 3, :], ps_t[:, 2 * NB:3 * NB], ALU.add))
            link(v.tensor_scalar(tie[:, 3, :], tie[:, 3, :], thr[:, 1:2], None, ALU.is_lt))
            link(v.tensor_tensor(tie[:, 3, :], tie[:, 3, :], tie[:, 1, :], ALU.mult))
            link(v.tensor_tensor(tie[:, 3, :], tie[:, 3, :], tie[:, 0, :], ALU.add))
            link(v.tensor_tensor(wsel[:, :], tie[:, 3, :], wts[:, :], ALU.mult))

            def finish_blocks(g, seconds):
                n = len(seconds)
                rows = [h[:, bass.ds(4 * g + q, 1), :].rearrange("p a d -> p (a d)") for q in range(n)]
                for q in range(n):
                    v.tensor_scalar(ybuf[:, q, :], rows[q], mneg[:, bass.ds(4 * g + q, 1)], rstd[:, bass.ds(4 * g + q, 1)],
                                    ALU.add, ALU.mult).then_inc(S["fin_steps"], 1)
                dve.wait_ge(S["fin_steps"], 12 * g + n)
                for q in range(n):
                    v.tensor_tensor(rows[q], rows[q], ybuf[:, q, :], ALU.add).then_inc(S["fin_steps"], 1)
                for q in range(n):
                    dve.wait_ge(S["y_done"], 4 * g + q + 1)
                    v.tensor_tensor(ybuf[:, 4 + q, :], seconds[q], bias_bc[:, 3, :], ALU.add).then_inc(S["fin_steps"], 1)
                dve.wait_ge(S["fin_steps"], 12 * g + 3 * n)
                for q in range(n):
                    v.scalar_tensor_tensor(out=rows[q], in0=ybuf[:, 4 + q, :], scalar=wsel[:, bass.ds(4 * g + q, 1)],
                                           in1=rows[q], op0=ALU.mult, op1=ALU.add).then_inc(S["fin_ready"], 1)
                dve.wait_ge(S["fin_ready"], 4 * g + n + 1)

            dve.wait_ge(S["y_out"], 4 * EARLY + 4)
            with dve.Fori(0, EARLY) as g:
                finish_blocks(g, [y_kept[:, bass.ds(4 * g + q, 1), :].rearrange("p a d -> p (a d)") for q in range(4)])
            with dve.Fori(EARLY, NB // 4) as g:
                finish_blocks(g, [bank[2 + q][:, 0:D] for q in range(4)])
            finish_blocks(NB // 4, [bank[2][:, 0:D]])

        @block.tensor
        def _(pe):
            te = nc.tensor
            pe.sem_inc(S["mm_done"], HALF)
            pe.sem_inc(S["turned"], 1)

            def count_chunk(n):
                d, c, W = n // 5, n % 5, HIST // 16
                pe.wait_ge(S["hot_ready"], 2 * n + 2)
                for k in range(W):
                    last = te.matmul(bank[d][:, 0:P], hot_hi[0:EP, n % 2, 16 * k:16 * k + 16, :].rearrange("p c v -> p (c v)"),
                                     hot_lo[0:EP, n % 2, 16 * k:16 * k + 16, :].rearrange("p c v -> p (c v)"),
                                     start=c == 0 and k == 0, stop=c == 4 and k == W - 1)
                last.then_inc(S["hist_chunk"], 1)

            def pick_counts(n):
                d = n // 2
                if n % 2 == 0:
                    pe.wait_ge(S["hist_masked"], d + 1)
                    te.matmul(bank[2][:, 0:64], hist_s[:, :], sel_hi, start=True, stop=True).then_inc(S["hist_sum"], 1)
                else:
                    pe.wait_ge(S["hist_picked"], d + 1)
                    te.matmul(bank[3][0:64, 0:1], hist_c[:, :], one, start=True, stop=True).then_inc(S["hist_total"], 1)

            def turn_block(n, odd):
                pe.wait_ge(S["xh_ready"], n + 1)
                for c in range(KC):
                    at = (odd * KC + c) * P
                    last = te.transpose(ps_t[:, at:at + P], xh[:, 1, c * P:(c + 1) * P], ident[:, :])
                last.then_inc(S["turned"], 1)

            def project_bank(n, k, odd):
                pe.wait_ge(S["proj_out"], PB * n + k + 1)
                for c in range(KC):
                    last = te.matmul(pj[k % 2][:, :], xts[:, odd, c, :], wrel[:, c, 2 * k:2 * k + 2, :].rearrange("p r o -> p (r o)"),
                                     start=c == 0, stop=c == KC - 1)
                last.then_inc(S["proj_done"], 1)

            def project(n, odd, between=None):
                pe.wait_ge(S["xt_ready"], n + 2)
                for k in range(PB):
                    if k == TURN_AT:
                        turn_block(n + 1, 1 - odd)
                    project_bank(n, k, odd)
                    if between is not None:
                        between(k)

            pe.wait_ge(S["pool_const"], 10)
            turn_block(0, 0)
            pe.wait_ge(S["wf_in"], KC * 16)
            for i in range(6):
                def count_between(k):
                    if i < 5 and k % 4 == 3:
                        count_chunk(2 * i + k // 4)
                    if i == 5 and k % 2 == 1:
                        pick_counts(k // 2)

                project(i, i % 2, count_between)
            with pe.Fori(3, (NB - 1) // 2) as j:
                for a in range(2):
                    project(2 * j + a, a)
            project(NB - 1, (NB - 1) % 2)

            def turn_keys(d, lanes, q, to):
                for c in range(4):
                    at = (4 * q + c) * P
                    last = te.transpose(to[:, c * P:(c + 1) * P], lanes[:, at:at + P], ident[:, :])
                last.then_inc(S["keys_out"], 1)

            pe.wait_ge(S["sorted_ready"], 1)
            for q in range(4):
                turn_keys(0, skeys[:, 0, :], q, bank[q])

            def sum_tile(i, t):
                half, s = t // HALF, t % HALF
                if s == 0:
                    pe.wait_ge(S["onehots_ready"], 2 * i + half + 1)
                pe.wait_ge(S["added"], TILES * i + t + (3 if t < 2 else 1))
                pe.wait_ge(gathered[s], 32 * i + 16 * half + 16)
                te.matmul(ring[t % 4][:, 0:D + 1], onehot[:, half, s, :], grow[:, s, :], start=True, stop=True).then_inc(S["mm_done"], 1)

            pe.wait_ge(S["wb_in"], KC * 16)
            pe.wait_ge(S["loop_in"], KC * 16)
            def forward_pass(i, odd, turn_next):
                n = i + NB
                pe.wait_ge(S["xt_ready"], n + 2)
                pe.wait_ge(S["h_ready"], 2 * i + 1)
                for c in range(KC):
                    last = te.matmul(ps_s[:, 0:D], xts[:, odd, c, :], loop_sb[:, c, :], start=c == 0, stop=c == KC - 1)
                last.then_inc(S["self_done"], 1)
                for t in range(2):
                    sum_tile(i, t)
                for k in range(PB):
                    if k == TURN_AT and turn_next:
                        turn_block(n + 1, 1 - odd)
                    project_bank(n, k, odd)
                    for t in range(2 + 4 * k, 2 + 4 * k + 4):
                        sum_tile(i, t)

            with pe.Fori(0, SPLIT // 2) as j:
                for a in range(2):
                    forward_pass(2 * j + a, (a + NB) % 2, True)
            pe.wait_ge(S["sorted_ready"], 2)
            pe.wait_ge(S["xt_ready"], SPLIT + NB + 2)
            for q in range(4):
                if q:
                    pe.wait_ge(S["keys_copied"], 4 + q)
                turn_keys(1, held[:, 0, :], q, ps_t)
            pe.wait_ge(S["keys_copied"], 8)
            with pe.Fori(SPLIT // 2, (NB - 1) // 2) as j:
                for a in range(2):
                    forward_pass(2 * j + a, (a + NB) % 2, True)
            forward_pass(NB - 1, (2 * NB - 1) % 2, False)
            with pe.Fori(PASSES, 2 * PASSES) as i:
                for t in range(TILES):
                    sum_tile(i, t)
            def router(i, odd):
                pe.wait_ge(S["xt2_ready"], i + 2)
                for k in range(KC):
                    last = te.matmul(ps_s[:, bass.ds(i, 1)], xts[:, odd, k, :], wr_sb[:, k:k + 1],
                                     start=k == 0, stop=k == KC - 1)
                last.then_inc(S["wt_done"], 1)

            def turn_late(i, odd):
                pe.wait_ge(S["xt2_ready"], i + 1)
                turn_block(i + 2 * NB, odd)

            def count_round(n):
                if n == 0:
                    pe.wait_ge(S["pool_const"], 13)
                pe.wait_ge(S["wt_ready"], n + 1)
                if n < 8:
                    te.matmul(ps_t[:, 0:WAYS], ones[:, :], cnt_f[:, 1, :], start=True, stop=True).then_inc(S["cnt_done"], 1)
                else:
                    te.matmul(ps_t[:, 0:2 * NB], ones[:, :], tie[:, 0:2, :].rearrange("p a b -> p (a b)"), start=True, stop=True)
                    te.matmul(ps_t[:, 2 * NB:3 * NB], tri[:, :], tie[:, 1, :], start=True, stop=True).then_inc(S["cnt_done"], 1)

            def ffn_group(g, blocks, between=None, early=True):
                for m in range(HC):
                    if m >= 2:
                        pe.wait_ge(S["hid_ready"], g * HC + m - 1)
                    for c in range(KC):
                        last = te.matmul(bank[m % 2][:, 0:blocks * P], w1_sb[:, c, m * P:(m + 1) * P],
                                         xt2[:, bass.ds(g * 4, blocks), c, :], start=c == 0, stop=c == KC - 1)
                    last.then_inc(S["hid_done"], 1)
                    if between is not None:
                        between(m)
                for q in range(blocks):
                    if early:
                        pe.wait_ge(S["y_out"], 4 * g + q + 1)
                    else:
                        pe.wait_ge(S["fin_ready"], 4 * (g - 1) + q + 2)
                    for m in range(HC):
                        if q == 0:
                            pe.wait_ge(S["hid_ready"], g * HC + m + 1)
                        last = te.matmul(bank[2 + q][:, 0:D], hid[:, m, q * P:(q + 1) * P], w2_sb[:, m, :],
                                         start=m == 0, stop=m == HC - 1)
                        if between is not None and m == HC // 2 - 1:
                            between(HC + 2 * q)
                    last.then_inc(S["y_done"], 1)
                    if between is not None:
                        between(HC + 2 * q + 1)

            for i in range(CHUNK + 1):
                if i < CHUNK:
                    turn_late(i, i % 2)
                if i > 0:
                    router(i - 1, (i - 1) % 2)
            pe.wait_ge(S["ffn_in"], 32)
            with pe.Fori(0, EARLY - 1) as g:
                def norm_next(n):
                    i = CHUNK + NORMS * g + n
                    if 1 < n <= NORMS + 1:
                        router(i - 2, (CHUNK + n) % 2)
                    if 0 < n <= NORMS:
                        turn_late(i - 1, (CHUNK + n - 1) % 2)

                ffn_group(g, 4, norm_next)
            ffn_group(EARLY - 1, 4, lambda n: count_round(n // 2) if n % 2 else None)
            count_round(8)
            ffn_group(EARLY, 4)
            with pe.Fori(EARLY + 1, NB // 4) as g:
                ffn_group(g, 4, early=False)
            ffn_group(NB // 4, 1, early=False)


INS = {"x": "x", "src": "src", "dst": "dst", "etype": "edge_type_16", "wf": "L0_gnn_Wf", "wb": "L0_gnn_Wb",
       "loop_w": "L0_gnn_loop_weight", "fwd_bias": "L0_gnn_forward_bias", "bwd_bias": "L0_gnn_backward_bias",
       "self_bias": "L0_gnn_self_bias", "wr": "L0_ffn_wr", "br": "L0_ffn_br", "w1": "L0_ffn_w1",
       "b1": "L0_ffn_b1", "w2": "L0_ffn_w2", "b2": "L0_ffn_b2"}


def kernel(**inputs):
    import concourse.bacc as bacc
    from concourse.bass_utils import run_bass_kernel_spmd

    nc = bacc.Bacc("TRN2", target_bir_lowering=False, num_devices=1)
    arrays, args = {}, {}
    for name, given in INS.items():
        a = np.ascontiguousarray(inputs[given])
        arrays[f"in_{name}"] = a
        args[name] = nc.dram_tensor(f"in_{name}", a.shape, mybir.dt.from_np(a.dtype), kind="ExternalInput").ap()
    n, d = inputs["x"].shape
    rels = inputs["L0_gnn_Wf"].shape[0]
    rows = -(-n // P) * P * rels
    for name in ("table_f", "table_b"):
        args[name] = nc.dram_tensor(name, (rows, d), F32).ap()
    args["x_self"] = nc.dram_tensor("x_self", (-(-n // P) * P, d), F32).ap()
    args["out"] = nc.dram_tensor("out_0", (n, d), F32, kind="ExternalOutput").ap()
    gnn_ffn_kernel(nc, **args)
    r = run_bass_kernel_spmd(nc, [arrays], core_ids=[0])
    return np.asarray(r.results[0]["out_0"])
```
